# Optimizing a Trainium2 kernel written in Bass

```python
import numpy as np
import jax
import jax.numpy as jnp

def _softmax(x, axis=-1):
    return jax.nn.softmax(x, axis=axis)

def _gelu(x):
    return jax.nn.gelu(x, approximate=True)

def _silu(x):
    return jax.nn.silu(x)

def _sigmoid(x):
    return jax.nn.sigmoid(x)

def _layernorm(x, axis=-1, eps=1e-05):
    m = jnp.mean(x, axis=axis, keepdims=True)
    v = jnp.var(x, axis=axis, keepdims=True)
    return (x - m) / jnp.sqrt(v + eps)

def _scatter_add(tgt, idx, src, axis=0):
    return tgt.at[idx].add(src)

def _segment_sum(src, seg, n):
    return jax.ops.segment_sum(src, seg, n)
kernel_name = 'mk_gnn_resnorm_d4_gnn_r8_cc3fd6'

def setup_inputs(seed: int=0):
    np.random.seed(seed)
    _w = jnp.asarray

    def _rec_inputs():
        import jax
        import jax.numpy as jnp
        _gk = jax.random.key(seed)
        x = -0.000202 + 1 * jax.random.normal(jax.random.fold_in(_gk, 1), (12500, 64), jnp.float32)
        _s = jax.random.randint(jax.random.fold_in(_gk, 2), (100000,), 0, 12500, jnp.int32)
        _d = jax.random.randint(jax.random.fold_in(_gk, 3), (100000,), 0, 12500, jnp.int32)
        _loop = jnp.arange(12500, dtype=jnp.int32)
        src = jnp.concatenate([_s, _d, _loop])
        dst = jnp.concatenate([_d, _s, _loop])
        _o = jnp.argsort(dst, stable=True)
        src = src[_o]
        dst = dst[_o]
        edge_attr_16 = 0.000196303 + 1.00016 * jax.random.normal(jax.random.fold_in(_gk, 12), (212500, 16), jnp.float32)
        return (x, src, dst, edge_attr_16)
    x, src, dst, edge_attr_16 = _rec_inputs()

    def _L0_gnn_setup():
        import jax, jax.numpy as jnp
        import numpy as np
        N = 12500
        E = 200000
        F_IN = 64
        H = 64
        L = 3
        key = jax.random.key(seed)
        ks = jax.random.split(key, 10)
        x = jax.random.normal(ks[0], (N, F_IN), jnp.float32)
        edge_index = jax.random.randint(ks[1], (2, E), 0, N, dtype=jnp.int64)
        s_in = 1.0 / np.sqrt(F_IN)
        s_h = 1.0 / np.sqrt(H)
        s_2h = 1.0 / np.sqrt(2 * H)
        W_in = jax.random.normal(ks[2], (F_IN, H), jnp.float32) * s_in
        b_in = jnp.zeros((H,), jnp.float32)
        l1_W = jax.random.normal(ks[3], (2 * H, H), jnp.float32) * s_2h
        l1_b = jnp.zeros((H,), jnp.float32)
        l2_W = jax.random.normal(ks[4], (H, 1), jnp.float32) * s_h
        l2_b = jnp.zeros((1,), jnp.float32)
        gcn_W = jax.random.normal(ks[5], (L, H, H), jnp.float32) * s_h
        gcn_b = jnp.zeros((L, H), jnp.float32)
        return {'x': x, 'edge_index': edge_index, 'W_in': W_in, 'b_in': b_in, 'l1_W': l1_W, 'l1_b': l1_b, 'l2_W': l2_W, 'l2_b': l2_b, 'gcn_W': gcn_W, 'gcn_b': gcn_b}
    _L0_gnn_all = _L0_gnn_setup()
    _L0_gnn_in = {k: v for k, v in _L0_gnn_all.items() if k in ('W_in', 'b_in', 'l1_W', 'l1_b', 'l2_W', 'l2_b', 'gcn_W', 'gcn_b')}
    del _L0_gnn_all

    def _L1_gnn_setup():
        import jax, jax.numpy as jnp
        import numpy as np
        N_NODES = 12500
        N_EDGES = 200000
        D_FEAT = 64
        key = jax.random.key(seed)
        k1, k2 = jax.random.split(key)
        x = jax.random.normal(k1, (N_NODES, D_FEAT), dtype=jnp.float32)
        edge_index = jax.random.randint(k2, (2, N_EDGES), 0, N_NODES, dtype=jnp.int64)
        return {'x': x, 'edge_index': edge_index}
    _L1_gnn_all = _L1_gnn_setup()
    _L1_gnn_in = {k: v for k, v in _L1_gnn_all.items() if k in ()}
    del _L1_gnn_all

    def _L2_gnn_setup():
        import jax, jax.numpy as jnp
        import numpy as np
        N_NODES = 12500
        N_EDGES = 200000
        NODE_DIM = 64
        EDGE_DIM = 16
        HIDDEN_DIM = 64
        key = jax.random.key(seed)
        ks = jax.random.split(key, 9)
        x = jax.random.normal(ks[0], (N_NODES, NODE_DIM), dtype=jnp.float32)
        edge_index = jax.random.randint(ks[1], (2, N_EDGES), 0, N_NODES, dtype=jnp.int32)
        edge_attr = jax.random.normal(ks[2], (N_EDGES, EDGE_DIM), dtype=jnp.float32)
        msg_in = 2 * NODE_DIM + EDGE_DIM
        s1 = 1.0 / np.sqrt(msg_in)
        s2 = 1.0 / np.sqrt(HIDDEN_DIM)
        su = 1.0 / np.sqrt(NODE_DIM + HIDDEN_DIM)
        W1 = jax.random.uniform(ks[3], (msg_in, HIDDEN_DIM), jnp.float32, -s1, s1)
        b1 = jax.random.uniform(ks[4], (HIDDEN_DIM,), jnp.float32, -s1, s1)
        W2 = jax.random.uniform(ks[5], (HIDDEN_DIM, HIDDEN_DIM), jnp.float32, -s2, s2)
        b2 = jax.random.uniform(ks[6], (HIDDEN_DIM,), jnp.float32, -s2, s2)
        Wu = jax.random.uniform(ks[7], (NODE_DIM + HIDDEN_DIM, NODE_DIM), jnp.float32, -su, su)
        bu = jax.random.uniform(ks[8], (NODE_DIM,), jnp.float32, -su, su)
        return {'x': x, 'edge_index': edge_index, 'edge_attr': edge_attr, 'W1': W1, 'b1': b1, 'W2': W2, 'b2': b2, 'Wu': Wu, 'bu': bu}
    _L2_gnn_all = _L2_gnn_setup()
    _L2_gnn_in = {k: v for k, v in _L2_gnn_all.items() if k in ('W1', 'b1', 'W2', 'b2', 'Wu', 'bu')}
    del _L2_gnn_all

    def _L3_gnn_setup():
        import jax, jax.numpy as jnp
        import numpy as np
        N_NODES = 6250
        N_EDGES = 100000
        D_FEAT = 64
        NEG_SLOPE = 0.01
        key = jax.random.key(seed)
        ks = jax.random.split(key, 8)
        in_feat = jax.random.normal(ks[0], (N_NODES, D_FEAT), dtype=jnp.float32)
        src = jax.random.randint(ks[1], (N_EDGES,), 0, N_NODES, dtype=jnp.int64)
        dst = jax.random.randint(ks[2], (N_EDGES,), 0, N_NODES, dtype=jnp.int64)
        scale = 1.0 / np.sqrt(D_FEAT)
        W1 = jax.random.normal(ks[3], (D_FEAT, D_FEAT), dtype=jnp.float32) * scale
        b1 = jnp.zeros((D_FEAT,), dtype=jnp.float32)
        W2 = jax.random.normal(ks[4], (D_FEAT, D_FEAT), dtype=jnp.float32) * scale
        b2 = jnp.zeros((D_FEAT,), dtype=jnp.float32)
        return {'in_feat': in_feat, 'W1': W1, 'b1': b1, 'W2': W2, 'b2': b2, 'src': src, 'dst': dst}
    _L3_gnn_all = _L3_gnn_setup()
    _L3_gnn_in = {k: v for k, v in _L3_gnn_all.items() if k in ('W1', 'b1', 'W2', 'b2')}
    del _L3_gnn_all
    return {'x': x, 'src': src, 'dst': dst, 'edge_attr_16': edge_attr_16, 'L0_gnn_W_in': _L0_gnn_in['W_in'], 'L0_gnn_b_in': _L0_gnn_in['b_in'], 'L0_gnn_l1_W': _L0_gnn_in['l1_W'], 'L0_gnn_l1_b': _L0_gnn_in['l1_b'], 'L0_gnn_l2_W': _L0_gnn_in['l2_W'], 'L0_gnn_l2_b': _L0_gnn_in['l2_b'], 'L0_gnn_gcn_W': _L0_gnn_in['gcn_W'], 'L0_gnn_gcn_b': _L0_gnn_in['gcn_b'], 'L2_gnn_W1': _L2_gnn_in['W1'], 'L2_gnn_b1': _L2_gnn_in['b1'], 'L2_gnn_W2': _L2_gnn_in['W2'], 'L2_gnn_b2': _L2_gnn_in['b2'], 'L2_gnn_Wu': _L2_gnn_in['Wu'], 'L2_gnn_bu': _L2_gnn_in['bu'], 'L3_gnn_W1': _L3_gnn_in['W1'], 'L3_gnn_b1': _L3_gnn_in['b1'], 'L3_gnn_W2': _L3_gnn_in['W2'], 'L3_gnn_b2': _L3_gnn_in['b2']}

def reference(x, src, dst, edge_attr_16, L0_gnn_W_in, L0_gnn_b_in, L0_gnn_l1_W, L0_gnn_l1_b, L0_gnn_l2_W, L0_gnn_l2_b, L0_gnn_gcn_W, L0_gnn_gcn_b, L2_gnn_W1, L2_gnn_b1, L2_gnn_W2, L2_gnn_b2, L2_gnn_Wu, L2_gnn_bu, L3_gnn_W1, L3_gnn_b1, L3_gnn_W2, L3_gnn_b2):
    import jax
    import jax.numpy as jnp

    def _L0_gnn_ref(x, edge_index, W_in, b_in, l1_W, l1_b, l2_W, l2_b, gcn_W, gcn_b):
        import jax, jax.numpy as jnp
        import numpy as np
        N = 12500
        E = 200000
        F_IN = 64
        H = 64
        L = 3
        emb0 = x @ W_in + b_in
        row, col = (edge_index[0], edge_index[1])
        A = emb0 @ l1_W[:H]
        B = emb0 @ l1_W[H:]
        h_edge = jax.nn.relu(A[row] + B[col] + l1_b)
        logit = (h_edge @ l2_W).reshape(-1) + l2_b[0]
        edge_mask = jax.nn.sigmoid(logit)
        outs = [emb0]
        h = emb0
        for li in range(L):
            msg = (h @ gcn_W[li])[row] * edge_mask[:, None]
            h = jax.ops.segment_sum(msg, col, num_segments=N) + gcn_b[li]
            if li < L - 1:
                h = jax.nn.relu(h)
            outs.append(h)
        emb_after = jnp.stack(outs, axis=1).mean(axis=1)
        return emb_after

    def _L1_gnn_ref(x, edge_index):
        import jax, jax.numpy as jnp
        import numpy as np
        N_NODES = 12500
        N_EDGES = 200000
        D_FEAT = 64
        from_, to_ = (edge_index[0], edge_index[1])
        n = x.shape[0]
        deg = jax.ops.segment_sum(jnp.ones_like(to_, dtype=x.dtype), to_, num_segments=n)
        deg_inv = jnp.where(deg > 0, 1.0 / jnp.sqrt(deg), 0.0)
        norm = deg_inv[from_] * deg_inv[to_]
        m_j = norm[:, None] * x[from_]
        out = jax.ops.segment_sum(m_j, to_, num_segments=n)
        return out

    def _L2_gnn_ref(x, edge_index, edge_attr, W1, b1, W2, b2, Wu, bu):
        import jax, jax.numpy as jnp
        import numpy as np
        N_NODES = 12500
        N_EDGES = 200000
        NODE_DIM = 64
        EDGE_DIM = 16
        HIDDEN_DIM = 64
        src, dst = (edge_index[0], edge_index[1])
        n_nodes = x.shape[0]
        edge_input = jnp.concatenate([x[src], x[dst], edge_attr], axis=1)
        h = jax.nn.relu(edge_input @ W1 + b1)
        messages = h @ W2 + b2
        aggregated = jax.ops.segment_sum(messages, dst, num_segments=n_nodes)
        counts = jax.ops.segment_sum(jnp.ones((messages.shape[0], 1), x.dtype), dst, num_segments=n_nodes)
        aggregated = aggregated / (counts + 1e-06)
        update_input = jnp.concatenate([x, aggregated], axis=1)
        x_new = jax.nn.relu(update_input @ Wu + bu)
        return x + x_new

    def _L3_gnn_ref(in_feat, W1, b1, W2, b2, src, dst):
        import jax, jax.numpy as jnp
        import numpy as np
        N_NODES = 6250
        N_EDGES = 100000
        D_FEAT = 64
        NEG_SLOPE = 0.01
        N = in_feat.shape[0]
        mask = (src != dst).astype(in_feat.dtype)
        out_deg = jax.ops.segment_sum(mask, src, num_segments=N) + 1.0
        in_deg = jax.ops.segment_sum(mask, dst, num_segments=N) + 1.0
        inv_out = jax.lax.rsqrt(out_deg)[:, None]
        inv_in = jax.lax.rsqrt(in_deg)[:, None]

        def layer(h, W, b):
            hs = h * inv_out
            msg = hs[src] * mask[:, None]
            agg = jax.ops.segment_sum(msg, dst, num_segments=N) + hs
            agg = agg * inv_in
            return jax.nn.leaky_relu(agg @ W + b, negative_slope=NEG_SLOPE)
        h = layer(in_feat, W1, b1)
        h = layer(h, W2, b2)
        return h
    edge_index = jnp.stack([src, dst])
    x = _layernorm(x + _L0_gnn_ref(x, edge_index, L0_gnn_W_in, L0_gnn_b_in, L0_gnn_l1_W, L0_gnn_l1_b, L0_gnn_l2_W, L0_gnn_l2_b, L0_gnn_gcn_W, L0_gnn_gcn_b), axis=-1)
    x = _layernorm(x + _L1_gnn_ref(x, edge_index), axis=-1)
    x = _layernorm(x + _L2_gnn_ref(x, edge_index, edge_attr_16, L2_gnn_W1, L2_gnn_b1, L2_gnn_W2, L2_gnn_b2, L2_gnn_Wu, L2_gnn_bu), axis=-1)
    x = _layernorm(x + _L3_gnn_ref(x, L3_gnn_W1, L3_gnn_b1, L3_gnn_W2, L3_gnn_b2, src, dst), axis=-1)
    return x

_drawn_inputs = setup_inputs


def setup_inputs(seed=0):
    import zlib

    import numpy as np

    out = dict(_drawn_inputs(seed))
    spreads = {'L0_gnn_b_in': (0.0, 0.1),
     'L0_gnn_l1_b': (0.0, 0.473),
     'L0_gnn_gcn_b': (0.0, 0.1),
     'L3_gnn_b1': (0.0, 0.1),
     'L3_gnn_b2': (0.0, 0.1)}
    factors = {'edge_attr_16': 25.78, 'L2_gnn_b1': 35.789, 'L2_gnn_b2': 4.867, 'L2_gnn_bu': 2.93}
    for name, (base, spread) in spreads.items():
        noise = np.random.default_rng([zlib.crc32(name.encode()), seed]).standard_normal(out[name].shape)
        drawn = base * np.exp(spread * noise) if base else spread * noise
        out[name] = jnp.asarray(drawn.astype(out[name].dtype))
    for name, factor in factors.items():
        out[name] = (out[name] * factor).astype(out[name].dtype)
    return out
```

```python
from contextlib import ExitStack

import concourse.bass as bass
from concourse import mybir

P = 128
F = 64
F32 = mybir.dt.float32
BF16 = mybir.dt.bfloat16
I32 = mybir.dt.int32
ALU = mybir.AluOpType
ACT = mybir.ActivationFunctionType
AX_X = mybir.AxisListType.X
ds = bass.ds

WIN = 128
TG = 8
SLOTS = 4
CH = 512
EPS = 1e-5
FAR = 1.0e6


def sizes(n_nodes, n_edges):
    np_ = -(-(n_nodes + WIN) // CH) * CH
    ng = -(-n_edges // (P * TG * SLOTS)) * SLOTS
    return np_, ng, ng + SLOTS


def gnn_kernel(nc, t, out):
    N, E = t["n_nodes"], t["n_edges"]
    NP, NG, NGP = sizes(N, E)
    NCH = NP // CH
    NB = CH // P
    HI = NP // P
    ITERS = NG // SLOTS
    GE = TG * P

    ctx = ExitStack()
    with ctx:
        def sb(name, shape, dt=F32):
            return ctx.enter_context(nc.sbuf_tensor(name, shape, dt))

        def ps(name, shape, dt=F32):
            return ctx.enter_context(nc.psum_tensor(name, shape, dt))

        def sem(name):
            return ctx.enter_context(nc.semaphore(name))

        def dram(name, shape):
            return nc.dram_tensor(name, shape, F32, kind="Internal").ap()

        tab_gate = dram("tab_gate", [NP, 2 * F])
        tab_dst = [dram("tab_dst0", [NP, F]), dram("tab_dst2", [NP, F])]
        tab = [None] + [dram(f"tab{n}", [NP, F]) for n in range(1, 7)]
        span_dram = dram("span_dram", [2, NG])

        acc = sb("acc", [F + 2, NP])
        x = sb("x", [F, NP])
        src = sb("src", [P, NGP * TG], I32)
        dst = sb("dst", [P, NGP * TG])
        dloc = sb("dloc", [P, NGP * TG])
        notself = sb("notself", [P, NGP * TG])
        gate = sb("gate", [P, NGP * TG])
        hist = sb("hist", [P, HI])
        inv_out = sb("inv_out", [P, HI])
        base = sb("base", [P, NGP + 1])
        base0 = sb("base0", [P, NG])
        base_i = sb("base_i", [P, NGP + 1], I32)
        span = sb("span", [P, NG])
        spanm = sb("spanm", [P, 1])
        rounds = sb("rounds", [P, 1], I32)
        low = sb("low", [NG // 2, 2])
        high = sb("high", [NG // 2, 2])
        pad_ok = sb("pad_ok", [P, TG])
        pad_far = sb("pad_far", [P, TG])
        zeros = sb("zeros", [F, CH])
        iota_i = sb("iota_i", [P, WIN], I32)
        iota = sb("iota", [P, WIN])
        eidx = sb("eidx", [P, TG], I32)
        ident = sb("ident", [P, P])
        center = sb("center", [F, F])
        center4 = sb("center4", [F, F])
        mean = sb("mean", [F, F])
        rowsel = sb("rowsel", [F + 2, 2, F])

        idx = sb("idx", [P, SLOTS, TG], I32)
        rows = sb("rows", [P, SLOTS, TG, 2 * F])
        hot = sb("hot", [P, SLOTS, TG, WIN])
        whot = sb("whot", [P, 2, TG, WIN])
        hotT = sb("hotT", [P, TG, P])
        pre = sb("pre", [P, TG, F])
        act_out = sb("act_out", [P, 2, TG, F])
        logit = sb("logit", [P, 2, TG])
        sig = sb("sig", [P, 2, TG])
        inwin = sb("inwin", [P, TG])
        onesm = sb("onesm", [P, 2, TG, 2])
        win = sb("win", [P, 2, F])
        attr_all = sb("attr_all", [P, 2 * GE])
        attr = attr_all[0:16, :].rearrange("p (h e) -> p h e", h=2)
        lo_hot = attr_all[:, 0:GE // 2].bitcast(BF16).rearrange("p (t n) -> p t n", n=P)
        hi_hot = attr_all[:, GE:GE + TG * HI // 2].bitcast(BF16).rearrange("p (t n) -> p t n", n=HI)
        lo_i = sb("lo_i", [P, TG], I32)
        hi_i = sb("hi_i", [P, TG], I32)
        lo = sb("lo", [P, TG])
        hi = sb("hi", [P, TG])

        w_in = sb("w_in", [F, F])
        wcat = sb("wcat", [F, 3 * F])
        gcn_w = sb("gcn_w", [F, 2, F])
        w1a = sb("w1a", [F, 2 * F])
        w1c = sb("w1c", [16, F])
        w2b = sb("w2b", [F + 2, F])
        wu = sb("wu", [F, 2, F])
        w3 = sb("w3", [F, 2, F])
        bcol = sb("bcol", [F, 7])
        l2w = sb("l2w", [P, F])
        l2b = sb("l2b", [P, 1])
        l1b = sb("l1b", [P, F])
        b1 = sb("b1", [P, F])

        def nodebuf(n):
            return hot[0:F, n // 2, (n % 2) * 4:(n % 2) * 4 + 4, :].rearrange("p a b -> p (a b)")
        emb, sq, var_e, std, rstd, degf, degm, dinv = (nodebuf(n) for n in range(8))
        tabsb = whot[:, 0, :, :].rearrange("p a b -> p (a b)")[:, 0:NB * 3 * F].rearrange("p (b c) -> p b c", b=NB)
        lnin = whot[0:F, 1, 4:8, :].rearrange("p a b -> p (a b)")
        xcopy = dinv
        rs2 = whot[0:F, 1, 0:4, :].rearrange("p a b -> p (a b)")

        ps_t = ps("ps_t", [P, 2 * 512])
        ps_e = ps("ps_e", [P, 2, 512])
        ps_a = ps("ps_a", [P, 2, 512])
        ps_h = ps("ps_h", [P, 512])
        ps_x = ps("ps_x", [P, 512])
        tT = ps_t[:, :].rearrange("p (b c) -> p b c", b=NB)

        s_w = sem("weights_loaded")
        s_x = sem("x_loaded")
        s_e = sem("edges_loaded")
        s_cst = sem("consts_made")
        s_span_out = sem("span_stored")
        s_span_in = sem("span_loaded")
        s_prep = sem("prep_done")
        s_rounds = sem("rounds_known")
        s_base = sem("base_ready")
        s_idx = sem("idx_ready")
        s_gather = [sem(f"gathered{n}") for n in range(SLOTS)]
        s_hot = sem("hot_ready")
        s_wh = sem("lhs_or_onehot_ready")
        s_tp = sem("transposed")
        s_tc = sem("hotT_copied")
        s_ex = sem("expanded")
        s_win = [sem("win_loaded0"), sem("win_loaded1")]
        s_attr = [sem("attr_loaded0"), sem("attr_loaded1")]
        s_logit = sem("logit_ready")
        s_sig = sem("sig_ready")
        s_pre = sem("pre_ready")
        s_relu = sem("relu_ready")
        s_agg = sem("agg_done")
        s_lohi = sem("lohi_ready")
        s_hist = sem("hist_done")
        s_histadd = sem("hist_added")
        s_accdone = sem("pass_summed")
        s_emb = sem("node_emb")
        s_h = sem("node_h")
        s_mm = sem("node_mm")
        s_passed = {e.engine: sem(f"waits_passed_{n}") for n, e in
                    (("pe", nc.tensor), ("act", nc.scalar), ("dve", nc.vector), ("pool", nc.gpsimd))}
        s_xcopy = sem("node_x_copied")
        s_leaky = sem("node_leaky")
        s_outroot = sem("out_degree_root")
        s_tabps = sem("node_tab_ps")
        s_tab = sem("node_tab_sb")
        s_stored = sem("node_tab_stored")
        s_xin = sem("ln_in")
        s_xc = sem("ln_centered")
        s_sq = sem("ln_squared")
        s_var = sem("ln_var")
        s_ve = sem("ln_var_eps")
        s_std = sem("ln_std")
        s_xn = sem("ln_out")
        s_deg = sem("deg_ps")
        s_degm = sem("deg_clamped")
        s_degs = sem("deg_sqrt")
        s_dinv = sem("dinv_ready")
        s_y = sem("scaled_ready")
        s_back = sem("hs_transposed_back")
        s_chunk = sem("chunk_done")
        s_out = sem("out_stored")

        block = ctx.enter_context(nc.Block())

        n_w = 21
        GATE, GCN1, GCN2, SUM, MLP, HOP1, HOP2 = range(7)
        PASSES = (GATE, GCN1, GCN2, SUM, MLP, HOP1, HOP2)
        DST_PASSES = (GATE, MLP)
        WEIGHTED = (GATE, GCN1, GCN2, SUM, HOP1, HOP2)

        def wait_apart(eng, name, value):
            eng.wait_ge(name, value)
            eng.sem_inc(s_passed[eng.engine], 1)

        def cols(c):
            return ds(c * CH, CH)

        def blk(c, b):
            return ds(c * CH + b * P, P)

        @block.sync
        def _(sp):
            def bc(ap, n):
                return ap.rearrange("(a n) -> a n", a=1).broadcast_to([P, n])
            l = [(w_in[:, :], t["L0_gnn_W_in"]), (wcat[:, 0:F], t["L0_gnn_l1_W"][0:F, :]),
                 (wcat[:, F:2 * F], t["L0_gnn_gcn_W"][0, :, :]), (wcat[:, 2 * F:], t["L0_gnn_l1_W"][F:2 * F, :]),
                 (gcn_w[:, 0, :], t["L0_gnn_gcn_W"][1, :, :]), (gcn_w[:, 1, :], t["L0_gnn_gcn_W"][2, :, :]),
                 (w1a[:, 0:F], t["L2_gnn_W1"][0:F, :]), (w1a[:, F:], t["L2_gnn_W1"][F:2 * F, :]),
                 (w1c[:, :], t["L2_gnn_W1"][2 * F:2 * F + 16, :]), (w2b[0:F, :], t["L2_gnn_W2"]),
                 (w2b[F:F + 1, :], t["L2_gnn_b2"].rearrange("(a n) -> a n", a=1)),
                 (wu[:, 0, :], t["L2_gnn_Wu"][0:F, :]), (wu[:, 1, :], t["L2_gnn_Wu"][F:2 * F, :]),
                 (w3[:, 0, :], t["L3_gnn_W1"]), (w3[:, 1, :], t["L3_gnn_W2"]),
                 (bcol[:, :], t["bias_cols"]),
                 (l2w[:, :], bc(t["L0_gnn_l2_W"].rearrange("a b -> (a b)"), F)), (l2b[:, :], bc(t["L0_gnn_l2_b"], 1)),
                 (l1b[:, :], bc(t["L0_gnn_l1_b"], F)), (b1[:, :], bc(t["L2_gnn_b1"], F))]
            sp.dma_start(x[:, :], t["xT"]).then_inc(s_x, 16)
            sp.dma_start(src[:, :], t["src_cols"]).then_inc(s_e, 16)
            sp.dma_start(dloc[:, :].bitcast(I32), t["dst_cols"]).then_inc(s_e, 16)
            sp.dma_start(rows[0:NG // 2, 0:2, :, :].rearrange("p a b c -> p (a b c)").bitcast(I32),
                         t["dst_groups"]).then_inc(s_e, 16)
            sp.wait_ge(s_cst, 1)
            for o, i in l:
                sp.dma_start(o, i).then_inc(s_w, 16)
            assert len(l) + 1 == n_w
            sp.wait_ge(s_prep, 1)
            sp.dma_start(span_dram[0, :].rearrange("(p k) -> p k", k=2), low[:, :]).then_inc(s_span_out, 16)
            sp.dma_start(span_dram[1, :].rearrange("(p k) -> p k", k=2), high[:, :]).then_inc(s_span_out, 16)
            sp.wait_ge(s_span_out, 32)
            sp.dma_start(base0[:, :], bc(span_dram[0, :], NG)).then_inc(s_span_in, 16)
            sp.dma_start(span[:, :], bc(span_dram[1, :], NG)).then_inc(s_span_in, 16)

        @block.gpsimd
        def _(pool):
            nc.gpsimd.memset(w2b[:, :], 0.0).then_inc(s_cst, 1)
            pool.wait_ge(s_cst, 1)
            nc.gpsimd.iota(iota_i[:, :], [[1, WIN]], base=0, channel_multiplier=0).then_inc(s_cst, 1)
            pool.wait_ge(s_cst, 2)
            nc.gpsimd.iota(eidx[:, :], [[P, TG]], base=(NG - SLOTS) * GE, channel_multiplier=1).then_inc(s_cst, 1)
            pool.wait_ge(s_cst, 3)
            nc.gpsimd.memset(ident[:, :], 0.0).then_inc(s_cst, 1)
            pool.wait_ge(s_cst, 4)
            nc.gpsimd.memset(mean[:, :], 1.0 / F).then_inc(s_cst, 1)
            pool.wait_ge(s_cst, 5)
            nc.gpsimd.memset(rowsel[:, :, :], 0.0).then_inc(s_cst, 1)
            pool.wait_ge(s_cst, 6)
            nc.gpsimd.affine_select(out=ident[:, :], in_=ident[:, :], compare_op=ALU.not_equal, fill=1.0, base=0,
                                    pattern=[[-1, P]], channel_multiplier=1).then_inc(s_cst, 1)
            pool.wait_ge(s_cst, 7)
            nc.gpsimd.affine_select(out=rowsel[:, :, :], in_=rowsel[:, :, :],
                                    compare_op=ALU.not_equal, fill=1.0, base=-F,
                                    pattern=[[-1, 2], [0, F]], channel_multiplier=1).then_inc(s_cst, 1)

            def store(nchunks, parts):
                n0 = store.done
                with pool.Fori(0, NCH) as c:
                    pool.wait_ge(s_tab, c + (n0 + 1))
                    for k, (tb, c0, wd) in enumerate(parts):
                        pool.dma_start(tb[ds(c * CH, CH), :].rearrange("(b p) f -> p b f", p=P),
                                       tabsb[:, :, c0:c0 + wd]).then_inc(s_store[k], 16)
                store.done += NCH
            store.done = 0
            s_store = [s_stored, s_out]

            def gathers(p, R):
                table = tab_gate if p == GATE else tab[p]
                width = 2 * F if p == GATE else F
                with pool.Fori(0, R) as r:
                    q = pool.snap(r + R * p)
                    with pool.Fori(0, ITERS) as i:
                        for u in range(SLOTS):
                            wait_apart(pool, s_idx, q * (NG + SLOTS) + i * SLOTS + (u + 1))
                            for j in range(TG):
                                nc.gpsimd.indirect_dma_start(
                                    rows[:, u, j, 0:width], None, table,
                                    bass.IndirectOffsetOnAxis(idx[:, u, j:j + 1], 0)).then_inc(s_gather[u], 16)

            pool.wait_ge(s_rounds, 1)
            R = pool.value_load(rounds[0:1, 0:1], min_val=1, max_val=NP // WIN)
            two = 0
            one = 0
            for p in PASSES:
                if p == GATE:
                    store(NCH, [(tab_gate, 0, 2 * F), (tab_dst[0], 2 * F, F)])
                    two += NCH
                elif p == MLP:
                    store(NCH, [(tab[p], 0, F), (tab_dst[1], F, F)])
                    two += NCH
                else:
                    store(NCH, [(tab[p], 0, F)])
                one += NCH
                pool.wait_ge(s_stored, 16 * one)
                pool.wait_ge(s_out, 16 * two)
                gathers(p, R)
            with pool.Fori(0, NCH) as c:
                pool.wait_ge(s_tab, c + (store.done + 1))
                pool.dma_start(out[ds(c * CH, CH), :].rearrange("(b p) f -> p b f", p=P),
                               tabsb[:, :, 0:F]).then_inc(s_stored, 16)
            pool.wait_ge(s_stored, 16 * (one + NCH))

        @block.tensor
        def _(pe):
            mm = nc.tensor.matmul
            pe.wait_ge(s_w, 16 * (n_w - 1))
            pe.wait_ge(s_cst, 8)
            pe.wait_ge(s_x, 16)
            pe.wait_ge(s_prep, 2)

            def dst_rows(p, i, u, r, kq):
                s = u % SLOTS
                k = i * SLOTS + u
                pe.wait_ge(s_hot, kq * (NG + 1) + k + 1)
                for j in range(TG):
                    last = nc.tensor.transpose(ps_t[:, j * P:(j + 1) * P], hot[:, s, j, :], ident[:, :])
                last.then_inc(s_tp, 1)
                pe.wait_ge(s_tc, kq * (NG + 1) + k + 1)
                nth = i * (SLOTS // 2) + (u // 2 + 1)
                pe.wait_ge(s_win[u % 2], (kq * (NG // 2 + 1) + nth) * 16)
                if p == MLP:
                    pe.wait_ge(s_attr[u % 2], (r * (NG // 2 + 1) + nth) * 16)
                for j in range(TG):
                    last = mm(ps_e[:, u % 2, j * F:(j + 1) * F], hotT[:, j, :], win[:, u % 2, :],
                              start=True, stop=p == GATE)
                    if p == MLP:
                        last = mm(ps_e[:, u % 2, j * F:(j + 1) * F], attr[:, u % 2, j * P:(j + 1) * P], w1c[:, :],
                                  start=False, stop=True)
                last.then_inc(s_ex, 1)

            def sums(p, i, u, r, q):
                k = i * SLOTS + u
                if p == GATE:
                    pe.wait_ge(s_wh, q * NG + k + 1)
                elif p == MLP:
                    pe.wait_ge(s_relu, r * NG + k + 1)
                else:
                    pe.wait_ge(s_wh, (r + R * WEIGHTED.index(p)) * NG + k + 1)
                    pe.wait_ge(s_gather[u], (q * ITERS + i + 1) * (16 * TG))
                for j in range(TG):
                    lhs = (rows[:, u, j, F:2 * F] if p == GATE else act_out[:, u % 2, j, :] if p == MLP
                           else rows[:, u, j, 0:F])
                    rhs = hot[:, u, j, :] if p == MLP else whot[:, u % 2, j, :]
                    last = mm(ps_a[0:F, u % 2, 0:WIN], lhs, rhs, start=j == 0, stop=j == TG - 1)
                if p == GATE:
                    for j in range(TG):
                        last = mm(ps_a[F:F + 2, u % 2, 0:WIN], onesm[:, u % 2, j, :], hot[:, u, j, :],
                                  start=j == 0, stop=j == TG - 1)
                last.then_inc(s_agg, 1)
                if p == GCN1:
                    pe.wait_ge(s_lohi, r * NG + k + 1)
                    for j in range(TG):
                        last = mm(ps_h[:, 0:HI], lo_hot[:, j, :], hi_hot[:, j, :], start=j == 0, stop=j == TG - 1)
                    last.then_inc(s_hist, 1)

            cnt = dict(emb=0, h=0, tab=0, chunk=0, xin=0, sq=0, deg=0, y=0, mm=0, dinv=0, tabsb=0)

            def to_table(c, inb, w, s_in, have, width):
                wait_apart(pe, s_in, c + (have + 1))
                for b in range(NB):
                    last = mm(tT[:, b, 0:width], inb[:, b * P:(b + 1) * P], w, start=True, stop=True)
                last.then_inc(s_tabps, 1)

            def norm(c, cmat):
                wait_apart(pe, s_xin, c + (cnt["xin"] + 1))
                mm(ps_e[0:F, 0, :], cmat, lnin, start=True, stop=True).then_inc(s_xc, 1)
                wait_apart(pe, s_sq, c + (cnt["xin"] + 1))
                mm(ps_e[0:F, 1, :], mean[:, :], sq, start=True, stop=True).then_inc(s_var, 1)

            def degs(c, which):
                mm(ps_a[0:F, 0, :], rowsel[:, which, :], acc[:, cols(c)],
                   start=True, stop=True).then_inc(s_deg, 1)

            R = None
            for p in PASSES:
                if p > 0:
                    wait_apart(pe, s_accdone, p)
                with pe.Fori(0, NCH) as c:
                    wait_apart(pe, s_chunk, c + (cnt["chunk"] + 1))
                    if p == GATE:
                        wait_apart(pe, s_xcopy, c + 1)
                        mm(ps_e[0:F, 0, :], w_in[:, :], xcopy, start=True, stop=True).then_inc(s_mm, 1)
                        to_table(c, emb, wcat[:, :], s_emb, cnt["emb"], 3 * F)
                    elif p in (GCN1, GCN2):
                        to_table(c, emb, gcn_w[:, p - 1, :], s_emb, cnt["emb"], F)
                    elif p == SUM:
                        norm(c, center4[:, :])
                        degs(c, 0)
                        to_table(c, emb, ident[0:F, 0:F], s_y, cnt["y"], F)
                    elif p == MLP:
                        degs(c, 0)
                        norm(c, center[:, :])
                        to_table(c, emb, w1a[:, :], s_xn, cnt["xin"], 2 * F)
                    elif p == HOP1:
                        mm(ps_a[0:F, 1, :], w2b[:, :], acc[:, cols(c)], start=True, stop=True).then_inc(s_mm, 1)
                        degs(c, 0)
                        wait_apart(pe, s_y, c + (cnt["y"] + 1))
                        wait_apart(pe, s_xcopy, c + (NCH + 1))
                        mm(ps_a[0:F, 1, :], wu[:, 0, :], xcopy, start=True, stop=False)
                        mm(ps_a[0:F, 1, :], wu[:, 1, :], emb, start=False, stop=True).then_inc(s_mm, 1)
                        norm(c, center[:, :])
                        to_table(c, emb, ident[0:F, 0:F], s_xn, cnt["xin"], F)
                    elif p == HOP2:
                        degs(c, 1)
                        wait_apart(pe, s_y, c + (cnt["y"] + 1))
                        mm(ps_a[0:F, 1, :], w3[:, 0, :], emb, start=True, stop=True).then_inc(s_mm, 1)
                        to_table(c, sq, ident[0:F, 0:F], s_leaky, 0, F)
                    if p in (HOP1, HOP2):
                        wait_apart(pe, s_tab, c + (cnt["tabsb"] + 1))
                        for b in range(NB):
                            last = mm(ps_x[0:F, b * P:(b + 1) * P], tabsb[:, b, 0:F], ident[:, :], start=True, stop=True)
                        last.then_inc(s_back, 1)
                cnt["chunk"] += NCH
                cnt["tabsb"] += NCH
                if p in (GATE, GCN1, GCN2):
                    cnt["emb"] += NCH
                if p in (SUM, MLP, HOP1):
                    cnt["xin"] += NCH
                if p in (SUM, HOP1, HOP2):
                    cnt["y"] += NCH
                if R is None:
                    pe.wait_ge(s_rounds, 1)
                    R = pe.value_load(rounds[0:1, 0:1], min_val=1, max_val=NP // WIN)
                with pe.Fori(0, R) as r:
                    q = pe.snap(r + R * p)
                    kq = pe.snap(r + R * DST_PASSES.index(p)) if p in DST_PASSES else None
                    if p in DST_PASSES:
                        dst_rows(p, 0, 0, r, kq)
                    with pe.Fori(0, ITERS) as i:
                        for u in range(SLOTS):
                            if p in DST_PASSES:
                                dst_rows(p, i, u + 1, r, kq)
                            sums(p, i, u, r, q)
            wait_apart(pe, s_accdone, len(PASSES))
            with pe.Fori(0, NCH) as c:
                wait_apart(pe, s_chunk, c + (cnt["chunk"] + 1))
                degs(c, 1)
                wait_apart(pe, s_y, c + (cnt["y"] + 1))
                mm(ps_a[0:F, 1, :], w3[:, 1, :], emb, start=True, stop=True).then_inc(s_mm, 1)
                norm(c, center[:, :])
                to_table(c, emb, ident[0:F, 0:F], s_xn, cnt["xin"], F)

        @block.scalar
        def _(act):
            A = nc.scalar.activation
            act.wait_ge(s_w, 16 * (n_w - 1))
            cnt = dict(mm=0, acc=0, xc=0, ve=0, deg=0, chunk=0)
            R = None

            def load_dst(p, b_load, u, n_expr):
                act.dma_start(win[:, u % 2, :], tab_dst[DST_PASSES.index(p)][ds(b_load, P), :]).then_inc(s_win[u % 2], 16)
                if p == MLP:
                    act.dma_start(attr[:, u % 2, :], t["attrT"][:, ds(n_expr * GE, GE)]).then_inc(s_attr[u % 2], 16)

            def norm(c):
                act.wait_ge(s_xc, c + (cnt["xc"] + 1))
                A(sq, ps_e[0:F, 0, :], ACT.Square).then_inc(s_sq, 1)
                act.wait_ge(s_ve, c + (cnt["xc"] + 1))
                A(std, var_e, ACT.Sqrt).then_inc(s_std, 1)

            def degsqrt(c):
                act.wait_ge(s_degm, c + (cnt["deg"] + 1))
                A(degm, degf, ACT.Sqrt).then_inc(s_degs, 1)

            for p in list(PASSES) + [len(PASSES)]:
                if p > 0:
                    act.wait_ge(s_accdone, p)
                if p == GCN2:
                    A(hist[:, :], hist[:, :], ACT.Sqrt).then_inc(s_outroot, 1)
                if p in (GATE, GCN1, GCN2, SUM, MLP, HOP1, HOP2) or p == len(PASSES):
                    with act.Fori(0, NCH) as c:
                        wait_apart(act, s_chunk, c + (cnt["chunk"] + 1))
                        if p in (GATE, HOP1):
                            A(xcopy, x[:, cols(c)], ACT.Copy).then_inc(s_xcopy, 1)
                        if p == GATE:
                            act.wait_ge(s_mm, c + 1)
                            A(emb, ps_e[0:F, 0, :], ACT.Identity, bias=bcol[:, 0:1]).then_inc(s_emb, 1)
                        elif p in (GCN1, GCN2):
                            A(emb, acc[0:F, cols(c)], ACT.Relu, bias=bcol[:, p:p + 1]).then_inc(s_emb, 1)
                        elif p == SUM:
                            norm(c)
                            degsqrt(c)
                        elif p == MLP:
                            degsqrt(c)
                            norm(c)
                        elif p == HOP1:
                            act.wait_ge(s_mm, c * 2 + (cnt["mm"] + 2))
                            A(sq, ps_a[0:F, 1, :], ACT.Relu, bias=bcol[:, 4:5]).then_inc(s_h, 1)
                            norm(c)
                        elif p == HOP2:
                            degsqrt(c)
                        else:
                            degsqrt(c)
                            norm(c)
                    cnt["chunk"] += NCH
                    if p == GATE:
                        cnt["mm"] += NCH
                    if p == HOP1:
                        cnt["mm"] += 2 * NCH
                    if p in (SUM, MLP, HOP1):
                        cnt["xc"] += NCH
                    if p in (SUM, MLP, HOP2):
                        cnt["deg"] += NCH
                if p == len(PASSES):
                    break
                if R is None:
                    act.wait_ge(s_rounds, 1)
                    R = act.value_load(rounds[0:1, 0:1], min_val=1, max_val=NP // WIN)
                if p not in DST_PASSES:
                    continue
                act.wait_ge(s_out, 16 * NCH * (DST_PASSES.index(p) + 1))
                with act.Fori(0, R) as r:
                    q = act.snap(r + R * p)
                    kq = act.snap(r + R * DST_PASSES.index(p))
                    wait_apart(act, s_base, q + 1)
                    for u in range(2):
                        b = act.value_load(base_i[0:1, 1 + u:2 + u], min_val=0, max_val=N)
                        load_dst(p, b, u, u)
                    act.wait_ge(s_tp, kq * (NG + 1) + 1)
                    A(hotT[:, :, :].rearrange("p a b -> p (a b)"), ps_t[:, :], ACT.Copy).then_inc(s_tc, 1)
                    with act.Fori(0, ITERS) as i:
                        for u in range(SLOTS):
                            k = i * SLOTS + u
                            b = act.value_load(base_i[0:1, ds(i * SLOTS + (u + 3), 1)], min_val=0, max_val=N)
                            act.wait_ge(s_ex, kq * (NG + 1) + k + 1)
                            load_dst(p, b, u, i * SLOTS + (u + 2))
                            act.wait_ge(s_tp, kq * (NG + 1) + k + 2)
                            A(hotT[:, :, :].rearrange("p a b -> p (a b)"), ps_t[:, :], ACT.Copy).then_inc(s_tc, 1)
                            if p == GATE:
                                act.wait_ge(s_logit, kq * NG + k + 1)
                                A(sig[:, u % 2, :], logit[:, u % 2, :], ACT.Sigmoid, bias=l2b[:, 0:1]).then_inc(s_sig, 1)
                            else:
                                act.wait_ge(s_pre, r * NG + k + 1)
                                A(act_out[:, u % 2, :, :], pre[:, :, :], ACT.Relu).then_inc(s_relu, 1)
                    for h in range(2):
                        act.wait_ge(s_win[h], (kq + 1) * (NG // 2 + 1) * 16)
                        if p == MLP:
                            act.wait_ge(s_attr[h], (r + 1) * ((NG // 2 + 1) * 16))

        @block.vector
        def _(dve):
            V = nc.vector
            dve.wait_ge(s_e, 48)
            g2 = rows[0:NG // 2, 0:2, :, :].rearrange("p a b c -> p a (b c)").bitcast(I32)
            V.tensor_reduce(low[:, :], g2, AX_X, ALU.min)
            V.tensor_reduce(high[:, :], g2, AX_X, ALU.max).then_inc(s_prep, 1)
            V.tensor_copy(dst[:, :], dloc[:, :].bitcast(I32))
            V.tensor_copy(gate[:, :], src[:, :])
            dve.drain()
            V.tensor_tensor(notself[:, :], gate[:, :], dst[:, :], ALU.not_equal)
            dve.drain()
            V.memset(gate[:, :], 0.0)
            dve.wait_ge(s_cst, 8)
            V.tensor_copy(iota[:, :], iota_i[:, :])
            for g in range(NG - SLOTS, NG):
                c0 = g * TG
                dve.drain()
                V.tensor_scalar(pad_ok[:, :], eidx[:, :], float(E - (g - (NG - SLOTS)) * GE), None, ALU.is_lt)
                dve.drain()
                V.tensor_scalar(pad_far[:, :], pad_ok[:, :], 1.0, FAR, ALU.subtract, ALU.mult)
                dve.drain()
                V.tensor_tensor(notself[:, c0:c0 + TG], notself[:, c0:c0 + TG], pad_ok[:, :], ALU.mult)
                V.tensor_tensor(dst[:, c0:c0 + TG], dst[:, c0:c0 + TG], pad_far[:, :], ALU.add)
            V.memset(dst[:, NG * TG:NGP * TG], -FAR)
            V.tensor_tensor(center[:, :], ident[0:F, 0:F], mean[:, :], ALU.subtract)
            dve.drain()
            V.tensor_scalar(center4[:, :], center[:, :], 0.25, None, ALU.mult)
            V.memset(onesm[:, :, :, :], 1.0)
            V.memset(base[:, :], 0.0)
            V.memset(zeros[:, :], 0.0)
            V.memset(acc[:, :], 0.0).then_inc(s_prep, 1)
            dve.drain()
            dve.wait_ge(s_span_in, 32)
            V.tensor_tensor(span[:, :], span[:, :], base0[:, :], ALU.subtract)
            dve.drain()
            V.tensor_reduce(spanm[:, :], span[:, :], AX_X, ALU.max)
            dve.drain()
            V.tensor_scalar(spanm[:, :], spanm[:, :], float(WIN), None, ALU.add)
            dve.drain()
            V.tensor_copy(rounds[:, :], spanm[:, :])
            dve.drain()
            V.tensor_scalar(rounds[:, :], rounds[:, :], WIN.bit_length() - 1, None, ALU.arith_shift_right)\
             .then_inc(s_rounds, 1)
            dve.wait_ge(s_w, 16 * (n_w - 1))
            dve.wait_ge(s_x, 16)
            dve.wait_ge(s_rounds, 1)
            R = dve.value_load(rounds[0:1, 0:1], min_val=1, max_val=NP // WIN)
            V.memset(inwin[:, 0:1], 0.0).then_inc(s_chunk, 1)

            cnt = dict(tab=0, xin=0, deg=0, emb=0, store=0, mm=0, h=0, back=0)

            def norm(c):
                dve.wait_ge(s_var, c + (cnt["xin"] + 1))
                V.tensor_scalar(var_e, ps_e[0:F, 1, :], EPS, None, ALU.add).then_inc(s_ve, 1)
                dve.wait_ge(s_std, c + (cnt["xin"] + 1))
                V.reciprocal(rstd, std)
                dve.drain()
                V.tensor_tensor(emb, ps_e[0:F, 0, :], rstd, ALU.mult).then_inc(s_xn, 1)
                dve.drain()
                V.tensor_copy(x[:, cols(c)], emb)

            def inv_sqrt_deg(c, plus):
                dve.wait_ge(s_deg, c + (cnt["deg_ps"] + 1))
                if plus:
                    V.tensor_scalar(degf, ps_a[0:F, 0, :], 1.0, None, ALU.add).then_inc(s_degm, 1)
                else:
                    V.tensor_scalar(degf, ps_a[0:F, 0, :], 1.0, None, ALU.max).then_inc(s_degm, 1)
                dve.wait_ge(s_degs, c + (cnt["deg"] + 1))
                V.reciprocal(dinv, degm)
                if not plus:
                    V.tensor_scalar(rs2, ps_a[0:F, 0, :], 1.0, None, ALU.min)
                    dve.drain()
                    V.tensor_tensor(dinv, dinv, rs2, ALU.mult)
            cnt["deg_ps"] = 0
            cnt["y"] = 0

            def table(c, width, bias=None, scale=False):
                dve.wait_ge(s_tabps, c + (cnt["tab"] + 1))
                o = tabsb[:, :, 0:width]
                if scale:
                    V.tensor_tensor(o, tT[:, :, 0:width],
                                    inv_out[:, ds(c * NB, NB)].rearrange("p (b a) -> p b a", a=1).broadcast_to([P, NB, width]),
                                    ALU.mult).then_inc(s_tab, 1)
                elif bias is None:
                    V.tensor_copy(o, tT[:, :, 0:width]).then_inc(s_tab, 1)
                else:
                    V.tensor_copy(tabsb[:, :, 0:width - F], tT[:, :, 0:width - F])
                    V.tensor_tensor(tabsb[:, :, width - F:width], tT[:, :, width - F:width],
                                    bias.rearrange("p (a f) -> p a f", a=1).broadcast_to([P, NB, F]), ALU.add).then_inc(s_tab, 1)

            two = [0]

            def stored(c, p):
                dve.wait_ge(s_stored, (c + (cnt["store"] + 1)) * 16)
                if p in DST_PASSES:
                    dve.wait_ge(s_out, (c + (two[0] + 1)) * 16)
                V.memset(inwin[:, 0:1], 0.0).then_inc(s_chunk, 1)

            def accadd(i, u, q, g_rows, b):
                V.tensor_tensor(acc[0:g_rows, ds(b, WIN)], acc[0:g_rows, ds(b, WIN)], ps_a[0:g_rows, u % 2, 0:WIN], ALU.add)

            def set_idx(k_expr, slot):
                V.tensor_copy(idx[:, slot, :], src[:, ds(k_expr, TG)]).then_inc(s_idx, 1)

            def onehot(o, k, weight=None):
                for j in range(TG):
                    if weight is None:
                        last = V.tensor_scalar(o[:, j, :], iota[:, :], dloc[:, ds(k * TG + j, 1)], None, ALU.is_equal)
                    else:
                        last = V.tensor_scalar(o[:, j, :], iota[:, :], dloc[:, ds(k * TG + j, 1)],
                                               weight[:, ds(k * TG + j, 1)], ALU.is_equal, ALU.mult)
                return last

            for p in list(PASSES) + [len(PASSES)]:
                if p == HOP1:
                    dve.wait_ge(s_outroot, 1)
                    V.reciprocal(inv_out[:, :], hist[:, :])
                with dve.Fori(0, NCH) as c:
                    dve.drain()
                    if p == GATE:
                        table(c, 3 * F, l1b[:, :])
                        V.scalar_tensor_tensor(x[:, cols(c)], x[:, cols(c)], 4.0, emb, ALU.mult, ALU.add)
                    elif p in (GCN1, GCN2):
                        table(c, F)
                        V.tensor_tensor(x[:, cols(c)], x[:, cols(c)], emb, ALU.add)
                        dve.drain()
                        V.tensor_copy(acc[0:F, cols(c)], zeros[:, :])
                    elif p == SUM:
                        V.scalar_tensor_tensor(lnin, acc[0:F, cols(c)], bcol[:, 3:4], x[:, cols(c)],
                                               ALU.add, ALU.add).then_inc(s_xin, 1)
                        norm(c)
                        inv_sqrt_deg(c, False)
                        dve.drain()
                        V.tensor_tensor(emb, x[:, cols(c)], dinv, ALU.mult).then_inc(s_y, 1)
                        table(c, F)
                        dve.drain()
                        V.tensor_copy(acc[0:F, cols(c)], zeros[:, :])
                    elif p == MLP:
                        inv_sqrt_deg(c, False)
                        dve.drain()
                        V.tensor_tensor(dinv, dinv, acc[0:F, cols(c)], ALU.mult)
                        dve.drain()
                        V.tensor_tensor(lnin, x[:, cols(c)], dinv, ALU.add).then_inc(s_xin, 1)
                        norm(c)
                        table(c, 2 * F, b1[:, :])
                        dve.drain()
                        V.tensor_copy(acc[0:F, cols(c)], zeros[:, :])
                    elif p == HOP1:
                        dve.wait_ge(s_mm, c * 2 + (cnt["mm"] + 1))
                        dve.wait_ge(s_deg, c + (cnt["deg_ps"] + 1))
                        V.tensor_scalar(degf, ps_a[0:F, 0, :], 1e-6, None, ALU.add)
                        dve.drain()
                        V.reciprocal(degm, degf)
                        dve.drain()
                        V.tensor_tensor(emb, ps_a[0:F, 1, :], degm, ALU.mult).then_inc(s_y, 1)
                        dve.wait_ge(s_h, c + 1)
                        V.scalar_tensor_tensor(lnin, x[:, cols(c)], 2.0, sq, ALU.mult, ALU.add).then_inc(s_xin, 1)
                        norm(c)
                        table(c, F, scale=True)
                        wait_apart(dve, s_back, c + (cnt["back"] + 1))
                        V.tensor_copy(acc[0:F, cols(c)], ps_x[0:F, :])
                    else:
                        inv_sqrt_deg(c, True)
                        dve.drain()
                        V.tensor_tensor(emb, acc[0:F, cols(c)], dinv, ALU.mult).then_inc(s_y, 1)
                        dve.wait_ge(s_mm, c + (cnt["mm"] + 1))
                        V.tensor_scalar(degf, ps_a[0:F, 1, :], bcol[:, p - 1:p], None, ALU.add)
                        if p == HOP2:
                            dve.drain()
                            V.scalar_tensor_tensor(sq, degf, 0.01, degf, ALU.mult, ALU.max).then_inc(s_leaky, 1)
                            table(c, F, scale=True)
                            wait_apart(dve, s_back, c + (cnt["back"] + 1))
                            V.tensor_copy(acc[0:F, cols(c)], ps_x[0:F, :])
                        else:
                            dve.drain()
                            V.scalar_tensor_tensor(rs2, degf, 0.01, degf, ALU.mult, ALU.max)
                            dve.drain()
                            V.tensor_tensor(lnin, x[:, cols(c)], rs2, ALU.add).then_inc(s_xin, 1)
                            norm(c)
                            table(c, F)
                    stored(c, p)
                cnt["tab"] += NCH
                cnt["store"] += NCH
                if p in DST_PASSES:
                    two[0] += NCH
                if p in (SUM, MLP, HOP1):
                    cnt["xin"] += NCH
                if p in (SUM, MLP, HOP2):
                    cnt["deg"] += NCH
                if p in (SUM, MLP, HOP1, HOP2):
                    cnt["deg_ps"] += NCH
                if p in (HOP1, HOP2):
                    cnt["back"] += NCH
                if p == GATE:
                    cnt["mm"] += NCH
                elif p == HOP1:
                    cnt["mm"] += 2 * NCH
                elif p == HOP2:
                    cnt["mm"] += NCH
                if p == len(PASSES):
                    break

                g_rows = F + 2 if p == GATE else F
                dve.drain()
                V.tensor_copy(base[:, 1:1 + NG], base0[:, :])
                with dve.Fori(0, R) as r:
                    q = dve.snap(r + R * p)
                    kq = dve.snap(r + R * DST_PASSES.index(p)) if p in DST_PASSES else None
                    dve.drain()
                    V.tensor_tensor(dloc[:, :].rearrange("p (g t) -> p g t", t=TG),
                                    dst[:, :].rearrange("p (g t) -> p g t", t=TG),
                                    base[:, 1:1 + NGP].rearrange("p (g a) -> p g a", a=1).broadcast_to([P, NGP, TG]),
                                    ALU.subtract)
                    dve.drain()
                    V.tensor_copy(base_i[:, :], base[:, :]).then_inc(s_base, 1)
                    if p == GCN1:
                        V.memset(hist[:, :], 0.0)
                    V.memset(ps_a[:, 1, 0:WIN], 0.0).then_inc(s_agg, 1)
                    for u in range(SLOTS - 1):
                        set_idx(u * TG, u)
                    if p in DST_PASSES:
                        onehot(hot[:, 0, :, :], 0).then_inc(s_hot, 1)
                    wait_apart(dve, s_base, q + 1)
                    with dve.Fori(0, ITERS) as i:
                        for u in range(SLOTS):
                            k = i * SLOTS + u
                            b = dve.value_load(base_i[0:1, ds(k, 1)], min_val=0, max_val=N)
                            if p in DST_PASSES:
                                onehot(hot[:, (u + 1) % SLOTS, :, :], k + 1).then_inc(s_hot, 1)
                                dve.wait_ge(s_ex, kq * (NG + 1) + k + 1)
                                dve.wait_ge(s_gather[u], (q * ITERS + i + 1) * (16 * TG))
                                if p == MLP:
                                    dve.wait_ge(s_agg, q * (NG + 1) + k + 1)
                                last = V.tensor_tensor(pre[:, :, :], ps_e[:, u % 2, :].rearrange("p (t f) -> p t f", f=F),
                                                rows[:, u, :, 0:F], ALU.add)
                                if p == MLP:
                                    last.then_inc(s_pre, 1)
                                else:
                                    dve.drain()
                                    V.scalar_tensor_tensor(pre[:, :, :], pre[:, :, :], 0.0,
                                                           l2w[:, :].rearrange("p (a f) -> p a f", a=1).broadcast_to([P, TG, F]),
                                                           ALU.max, ALU.mult)
                                    dve.drain()
                                    V.tensor_reduce(logit[:, u % 2, :], pre[:, :, :], AX_X, ALU.add).then_inc(s_logit, 1)
                            dve.drain()
                            dve.wait_ge(s_agg, q * (NG + 1) + k + 1)
                            V.tensor_tensor(acc[0:g_rows, ds(b, WIN)], acc[0:g_rows, ds(b, WIN)],
                                            ps_a[0:g_rows, (u - 1) % 2, 0:WIN], ALU.add)
                            set_idx((k + SLOTS - 1) * TG, (u - 1) % SLOTS)
                            if p == GATE:
                                kk = k * TG
                                V.tensor_copy(onesm[:, u % 2, :, 1], notself[:, ds(kk, TG)])
                                V.tensor_scalar(inwin[:, :], dloc[:, ds(kk, TG)], 0.0, None, ALU.is_ge)
                                dve.drain()
                                V.scalar_tensor_tensor(inwin[:, :], dloc[:, ds(kk, TG)], float(WIN), inwin[:, :],
                                                       ALU.is_lt, ALU.mult)
                                dve.drain()
                                dve.wait_ge(s_sig, kq * NG + k + 1)
                                V.tensor_tensor(inwin[:, :], inwin[:, :], sig[:, u % 2, :], ALU.mult)
                                dve.drain()
                                V.tensor_tensor(gate[:, ds(kk, TG)], gate[:, ds(kk, TG)], inwin[:, :], ALU.add)
                                V.tensor_tensor(whot[:, u % 2, :, :], hot[:, u, :, :],
                                                sig[:, u % 2, :].rearrange("p (t a) -> p t a", a=1).broadcast_to([P, TG, WIN]),
                                                ALU.mult).then_inc(s_wh, 1)
                            elif p != MLP:
                                w = {GCN1: gate, GCN2: gate, SUM: None, HOP1: notself, HOP2: notself}[p]
                                onehot(whot[:, u % 2, :, :], k, w).then_inc(s_wh, 1)
                            if p == GCN1:
                                kk = k * TG
                                V.tensor_scalar(lo_i[:, :], src[:, ds(kk, TG)], P - 1, None, ALU.bitwise_and)
                                V.tensor_scalar(hi_i[:, :], src[:, ds(kk, TG)], P.bit_length() - 1, None, ALU.arith_shift_right)
                                dve.drain()
                                V.tensor_copy(lo[:, :], lo_i[:, :])
                                V.tensor_scalar(hi[:, :], notself[:, ds(kk, TG)], -1.0, -float(HI), ALU.add, ALU.mult)
                                dve.drain()
                                V.tensor_tensor(hi[:, :], hi[:, :], hi_i[:, :], ALU.add)
                                dve.drain()
                                V.tensor_tensor(lo_hot[:, :, :], iota[:, 0:P].rearrange("p (a n) -> p a n", a=1).broadcast_to([P, TG, P]),
                                                lo[:, :].rearrange("p (t a) -> p t a", a=1).broadcast_to([P, TG, P]), ALU.is_equal)
                                V.tensor_tensor(hi_hot[:, :, :], iota[:, 0:HI].rearrange("p (a n) -> p a n", a=1).broadcast_to([P, TG, HI]),
                                                hi[:, :].rearrange("p (t a) -> p t a", a=1).broadcast_to([P, TG, HI]), ALU.is_equal)\
                                 .then_inc(s_lohi, 1)
                                dve.wait_ge(s_hist, r * NG + k + 1)
                                V.tensor_tensor(hist[:, :], hist[:, :], ps_h[:, 0:HI], ALU.add)
                    b = dve.value_load(base_i[0:1, NG:NG + 1], min_val=0, max_val=N)
                    dve.drain()
                    dve.wait_ge(s_agg, (q + 1) * (NG + 1))
                    V.tensor_tensor(acc[0:g_rows, ds(b, WIN)], acc[0:g_rows, ds(b, WIN)],
                                    ps_a[0:g_rows, (SLOTS - 1) % 2, 0:WIN], ALU.add)
                    V.tensor_copy(idx[:, SLOTS - 1, :], src[:, 0:TG]).then_inc(s_idx, 1)
                    dve.drain()
                    V.tensor_scalar(base[:, 1:1 + NG], base[:, 1:1 + NG], float(WIN), float(N), ALU.add, ALU.min)
                if p == GCN1:
                    dve.drain()
                    V.tensor_scalar(hist[:, :], hist[:, :], 1.0, None, ALU.add)
                V.memset(inwin[:, 0:1], 0.0).then_inc(s_accdone, 1)


_W = ["L0_gnn_W_in", "L0_gnn_l1_W", "L0_gnn_l1_b", "L0_gnn_l2_W", "L0_gnn_l2_b", "L0_gnn_gcn_W",
      "L2_gnn_W1", "L2_gnn_b1", "L2_gnn_W2", "L2_gnn_b2", "L2_gnn_Wu", "L3_gnn_W1", "L3_gnn_W2"]


def kernel(**inputs):
    import numpy as np
    import concourse.bacc as bacc
    from concourse.bass_utils import run_bass_kernel_spmd

    a = {k: np.asarray(v) for k, v in inputs.items()}
    n, e = a["x"].shape[0], a["src"].shape[0]
    np_, ng, ngp = sizes(n, e)
    per = TG * P

    def cols(v, m, mode):
        return np.ascontiguousarray(np.pad(v, (0, m * per - e), mode=mode).reshape(-1, P).T)

    xT = np.zeros((F, np_), a["x"].dtype)
    xT[:, :n] = a["x"].T
    attrT = np.zeros((a["edge_attr_16"].shape[1], ngp * per), a["edge_attr_16"].dtype)
    attrT[:, :e] = a["edge_attr_16"].T
    arrays = {k: np.ascontiguousarray(a[k]) for k in _W}
    arrays["xT"] = xT
    arrays["attrT"] = attrT
    arrays["src_cols"] = cols(a["src"], ngp, "constant")
    arrays["dst_cols"] = cols(a["dst"], ngp, "edge")
    arrays["dst_groups"] = np.pad(a["dst"], (0, ng * per - e), mode="edge").reshape(ng // 2, 2 * per)
    arrays["bias_cols"] = np.ascontiguousarray(np.stack(
        [a["L0_gnn_b_in"], *a["L0_gnn_gcn_b"], a["L2_gnn_bu"], a["L3_gnn_b1"], a["L3_gnn_b2"]], axis=1))

    nc = bacc.Bacc("TRN2", target_bir_lowering=False, num_devices=1)
    t = {k: nc.dram_tensor(f"in_{k}", v.shape, mybir.dt.from_np(v.dtype), kind="ExternalInput").ap()
         for k, v in arrays.items()}
    t["n_nodes"], t["n_edges"] = n, e
    out = nc.dram_tensor("out_0", (np_, F), F32, kind="ExternalOutput").ap()
    gnn_kernel(nc, t, out)
    r = run_bass_kernel_spmd(nc, [{f"in_{k}": v for k, v in arrays.items()}], core_ids=[0])
    return r.results[0]["out_0"][:n]
```

```python
from contextlib import ExitStack

import concourse.bass as bass
from concourse import mybir

P = 128
F = 64
F32 = mybir.dt.float32
BF16 = mybir.dt.bfloat16
I32 = mybir.dt.int32
ALU = mybir.AluOpType
ACT = mybir.ActivationFunctionType
AX_X = mybir.AxisListType.X
ds = bass.ds

WIN = 128
TG = 8
SLOTS = 4
CH = 512
EPS = 1e-5
CHAINS = 4
ROWS = 98
FAR = 1.0e6


def sizes(n_nodes, n_edges):
    np_ = -(-(n_nodes + WIN) // CH) * CH
    ng = -(-n_edges // (P * TG * SLOTS)) * SLOTS
    return np_, ng, ng + SLOTS


def gnn_kernel(nc, t, out):
    N, E = t["n_nodes"], t["n_edges"]
    NP, NG, NGP = sizes(N, E)
    NCH = NP // CH
    NB = CH // P
    HI = NP // P
    ITERS = NG // SLOTS
    GE = TG * P
    SLICE = 256
    SLICES = NP // SLICE
    assert SLICES <= ITERS

    ctx = ExitStack()
    with ctx:
        def sb(name, shape, dt=F32):
            return ctx.enter_context(nc.sbuf_tensor(name, shape, dt))

        def ps(name, shape, dt=F32):
            return ctx.enter_context(nc.psum_tensor(name, shape, dt))

        def sem(name):
            return ctx.enter_context(nc.semaphore(name))

        def dram(name, shape):
            return nc.dram_tensor(name, shape, F32, kind="Internal").ap()

        tab_gate = dram("tab_gate", [NP, 2 * F])
        tab_dst = [dram("tab_dst0", [NP, F]), dram("tab_dst2", [NP, F])]
        tab = [None] + [dram(f"tab{n}", [NP, F]) for n in range(1, 7)]
        span_dram = dram("span_dram", [2, NG])

        acc = sb("acc", [P, NP])
        x = sb("x", [P, NP])
        src = sb("src", [P, NGP * TG], I32)
        dst = sb("dst", [P, NGP * TG])
        dloc = sb("dloc", [P, NGP * TG])
        notself = sb("notself", [P, NGP * TG])
        gate = sb("gate", [P, NGP * TG])
        hist = sb("hist", [P, HI])
        inv_out = sb("inv_out", [P, HI])
        base = sb("base", [P, NGP + 1])
        base0 = sb("base0", [P, NG])
        base_i = sb("base_i", [P, NGP + 1], I32)
        span = sb("span", [P, NG])
        spanm = sb("spanm", [P, 1])
        rounds = sb("rounds", [P, 1], I32)
        low = sb("low", [NG // 2, 2])
        high = sb("high", [NG // 2, 2])
        pad_ok = sb("pad_ok", [P, TG])
        pad_far = sb("pad_far", [P, TG])
        zeros = sb("zeros", [F, CH])
        two_i = sb("two_i", [P, 1], I32)
        iota_i = sb("iota_i", [P, WIN], I32)
        iota = sb("iota", [P, WIN])
        eidx = sb("eidx", [P, TG], I32)
        ident = sb("ident", [P, P])
        center = sb("center", [F, F])
        center4 = sb("center4", [F, F])
        mean = sb("mean", [F, F])
        rowsel = sb("rowsel", [ROWS, 2, F])
        rowsel_x = sb("rowsel_x", [F + 1, F])
        plus = sb("plus", [P, 1])
        eps_col = sb("eps_col", [F, 1])

        token = sb("token", [1, CHAINS])
        idx = sb("idx", [P, SLOTS, TG], I32)
        rows = sb("rows", [P, SLOTS, TG, 2 * F])
        hot = sb("hot", [P, SLOTS, TG, WIN])
        whot = sb("whot", [P, 2, TG, WIN])
        hotT = sb("hotT", [P, TG, P])
        pre = sb("pre", [P, TG, F])
        act_out = sb("act_out", [P, 2, TG, F])
        logit = sb("logit", [P, 2, TG])
        sig = sb("sig", [P, 2, TG])
        inwin = sb("inwin", [P, TG])
        onesm = sb("onesm", [P, 2, TG, 2])
        win = sb("win", [P, 2, F])
        attr_all = sb("attr_all", [P, 2 * GE])
        attr = attr_all[0:16, :].rearrange("p (h e) -> p h e", h=2)
        lo_hot = attr_all[:, 0:GE // 2].bitcast(BF16).rearrange("p (t n) -> p t n", n=P)
        hi_hot = attr_all[:, GE:GE + TG * HI // 2].bitcast(BF16).rearrange("p (t n) -> p t n", n=HI)
        lo_i = sb("lo_i", [P, TG], I32)
        hi_i = sb("hi_i", [P, TG], I32)
        lo = sb("lo", [P, TG])
        hi = sb("hi", [P, TG])

        w_in = sb("w_in", [F, F])
        wcat = sb("wcat", [F, 3 * F])
        gcn_w = sb("gcn_w", [F, 2, F])
        w1a = sb("w1a", [F, 2 * F])
        w1c = sb("w1c", [16, F])
        w2b = sb("w2b", [F + 2, F])
        wu = sb("wu", [F, 2, F])
        w3 = sb("w3", [F, 2, F])
        bcol = sb("bcol", [F, 7])
        l2w = sb("l2w", [P, F])
        l2b = sb("l2b", [P, 1])
        l1b = sb("l1b", [P, F])
        b1 = sb("b1", [P, F])

        def halves(ring, slots):
            return [ring[:, n, h:h + TG // 2, :].rearrange("p a b -> p (a b)")
                    for n in range(slots) for h in (0, TG // 2)]
        spare = halves(hot, SLOTS) + halves(rows, SLOTS) + halves(whot, 2)
        assert len(spare) >= 5 * CHAINS and TG * P == 2 * CH
        E_, S_, V_, L_, X_ = ([spare[b * CHAINS + w][0:F, :] for w in range(CHAINS)] for b in range(5))
        T_ = [a[:, 0:NB * 3 * F].rearrange("p (b c) -> p b c", b=NB) for a in
              (hotT[:, :, :].rearrange("p a b -> p (a b)"), attr_all[:, 0:GE], attr_all[:, GE:2 * GE],
               act_out[:, :, :, :].rearrange("p a b c -> p (a b c)"))]

        ps_t = ps("ps_t", [P, 2 * 512])
        ps_e = ps("ps_e", [P, 2, 512])
        ps_a = ps("ps_a", [P, 2, 512])
        ps_hx = ps("ps_hx", [P, 2, 512])
        ps_h = ps_hx[:, 0, :]
        A_ = [ps_t[:, 0:512], ps_e[:, 0, :], ps_a[:, 0, :], ps_hx[:, 0, :]]
        B_ = [ps_t[:, 512:1024], ps_e[:, 1, :], ps_a[:, 1, :], ps_hx[:, 1, :]]

        def blocks(bank, width):
            return bank[:, 0:NB * width].rearrange("p (b c) -> p b c", b=NB)

        s_w = sem("weights_loaded")
        s_x = sem("x_loaded")
        s_e = sem("edges_loaded")
        s_cst = sem("consts_made")
        s_span_out = sem("span_stored")
        s_span_in = sem("span_loaded")
        s_prep = sem("prep_done")
        s_rounds = sem("rounds_known")
        s_base = sem("base_ready")
        s_idx = sem("idx_ready")
        s_gather = [sem(f"gathered{n}") for n in range(SLOTS)]
        s_hot = sem("hot_ready")
        s_wh = sem("lhs_or_onehot_ready")
        s_tp = sem("transposed")
        s_tc = sem("hotT_copied")
        s_ex = sem("expanded")
        s_win = [sem("win_loaded0"), sem("win_loaded1")]
        s_attr = [sem("attr_loaded0"), sem("attr_loaded1")]
        s_logit = sem("logit_ready")
        s_sig = sem("sig_ready")
        s_pre = sem("pre_ready")
        s_relu = sem("relu_ready")
        s_agg = sem("agg_done")
        s_lohi = sem("lohi_ready")
        s_hist = sem("hist_done")
        s_histadd = sem("hist_added")
        s_accdone = sem("pass_summed")
        s_xcopy = sem("node_x_copied")
        s_emb = sem("node_emb")
        s_row = sem("node_row_spread")
        s_agg0 = sem("node_aggregate")
        s_mm = sem("node_product")
        s_mm2 = sem("node_update_product")
        s_h = sem("node_relu")
        s_leaky = sem("node_leaky")
        s_xin = sem("ln_in")
        s_xc = sem("ln_centered")
        s_sq = sem("ln_squared")
        s_var = sem("ln_var")
        s_std = sem("ln_std")
        s_y = sem("table_in")
        s_tabps = sem("node_tab_ps")
        s_tab = sem("node_tab_sb")
        s_back = sem("hs_transposed_back")
        s_chunk = sem("chunk_done")
        s_stored = [sem(f"tab_stored{w}") for w in range(CHAINS)]
        s_stored2 = [sem(f"dst_tab_stored{w}") for w in range(CHAINS)]
        s_deg = sem("deg_clamped")
        s_root = sem("deg_rooted")
        s_outroot = sem("out_degree_root")
        s_passed = {e.engine: sem(f"waits_passed_{n}") for n, e in
                    (("pe", nc.tensor), ("act", nc.scalar), ("dve", nc.vector), ("pool", nc.gpsimd))}

        block = ctx.enter_context(nc.Block())

        n_w = 21
        GATE, GCN1, GCN2, SUM, MLP, HOP1, HOP2 = range(7)
        PASSES = (GATE, GCN1, GCN2, SUM, MLP, HOP1, HOP2)
        END = len(PASSES)
        DST_PASSES = (GATE, MLP)
        WEIGHTED = (GATE, GCN1, GCN2, SUM, HOP1, HOP2)

        MADE = {
            s_xcopy: (GATE, HOP1), s_emb: (GATE, GCN1, GCN2), s_row: (SUM, MLP, HOP1, HOP2, END), s_agg0: (HOP1, END),
            s_mm: (GATE, HOP1, HOP2, END), s_mm2: (HOP1,), s_h: (HOP1,), s_leaky: (HOP2,),
            s_xin: (SUM, MLP, HOP1, END), s_xc: (SUM, MLP, HOP1, END), s_sq: (SUM, MLP, HOP1, END),
            s_var: (SUM, MLP, HOP1, END), s_std: (SUM, MLP, HOP1, END),
            s_y: (SUM, MLP, HOP1, HOP2, END), s_tabps: (GATE,) + PASSES[1:] + (END,),
            s_tab: (GATE,) + PASSES[1:] + (END,), s_back: (HOP1, HOP2), s_chunk: (GATE,) + PASSES[1:] + (END,),
        }

        def made(name, p, c):
            return c + (sum(NCH for q in MADE[name] if q < p) + 1)

        def chains(eng, body):
            def step(first, n, nth):
                turns = [body(first + w, w, nth) for w in range(n)]
                while turns:
                    turns = [g for g in turns if next(g, body) is not body]
            with eng.Fori(0, NCH // CHAINS) as i:
                step(i * CHAINS, CHAINS, i)
            if NCH % CHAINS:
                step(NCH // CHAINS * CHAINS, NCH % CHAINS, NCH // CHAINS)

        def turns_of(w):
            return (NCH - w + CHAINS - 1) // CHAINS

        def wait_apart(eng, name, value):
            eng.wait_ge(name, value)
            eng.sem_inc(s_passed[eng.engine], 1)

        def cols(c):
            return ds(c * CH, CH)

        def blk(c, b):
            return ds(c * CH + b * P, P)

        @block.sync
        def _(sp):
            def bc(ap, n):
                return ap.rearrange("(a n) -> a n", a=1).broadcast_to([P, n])
            l = [(w_in[:, :], t["L0_gnn_W_in"]), (wcat[:, 0:F], t["L0_gnn_l1_W"][0:F, :]),
                 (wcat[:, F:2 * F], t["L0_gnn_gcn_W"][0, :, :]), (wcat[:, 2 * F:], t["L0_gnn_l1_W"][F:2 * F, :]),
                 (gcn_w[:, 0, :], t["L0_gnn_gcn_W"][1, :, :]), (gcn_w[:, 1, :], t["L0_gnn_gcn_W"][2, :, :]),
                 (w1a[:, 0:F], t["L2_gnn_W1"][0:F, :]), (w1a[:, F:], t["L2_gnn_W1"][F:2 * F, :]),
                 (w1c[:, :], t["L2_gnn_W1"][2 * F:2 * F + 16, :]), (w2b[0:F, :], t["L2_gnn_W2"]),
                 (w2b[F:F + 1, :], t["L2_gnn_b2"].rearrange("(a n) -> a n", a=1)),
                 (wu[:, 0, :], t["L2_gnn_Wu"][0:F, :]), (wu[:, 1, :], t["L2_gnn_Wu"][F:2 * F, :]),
                 (w3[:, 0, :], t["L3_gnn_W1"]), (w3[:, 1, :], t["L3_gnn_W2"]),
                 (bcol[:, :], t["bias_cols"]),
                 (l2w[:, :], bc(t["L0_gnn_l2_W"].rearrange("a b -> (a b)"), F)), (l2b[:, :], bc(t["L0_gnn_l2_b"], 1)),
                 (l1b[:, :], bc(t["L0_gnn_l1_b"], F)), (b1[:, :], bc(t["L2_gnn_b1"], F))]
            sp.dma_start(x[0:F, :], t["xT"]).then_inc(s_x, 16)
            sp.dma_start(src[:, :], t["src_cols"]).then_inc(s_e, 16)
            sp.dma_start(dloc[:, :].bitcast(I32), t["dst_cols"]).then_inc(s_e, 16)
            sp.dma_start(rows[0:NG // 2, 0:2, :, :].rearrange("p a b c -> p (a b c)").bitcast(I32),
                         t["dst_groups"]).then_inc(s_e, 16)
            sp.wait_ge(s_cst, 1)
            for o, i in l:
                sp.dma_start(o, i).then_inc(s_w, 16)
            assert len(l) + 1 == n_w
            sp.wait_ge(s_prep, 1)
            sp.dma_start(span_dram[0, :].rearrange("(p k) -> p k", k=2), low[:, :]).then_inc(s_span_out, 16)
            sp.dma_start(span_dram[1, :].rearrange("(p k) -> p k", k=2), high[:, :]).then_inc(s_span_out, 16)
            sp.wait_ge(s_span_out, 32)
            sp.dma_start(base0[:, :], bc(span_dram[0, :], NG)).then_inc(s_span_in, 16)
            sp.dma_start(span[:, :], bc(span_dram[1, :], NG)).then_inc(s_span_in, 16)

            for p in PASSES + (END,):
                def body(c, w, nth, p=p):
                    table = tab_gate if p == GATE else out if p == END else tab[p]
                    width = 2 * F if p == GATE else F
                    sp.wait_ge(s_tab, made(s_tab, p, c))
                    sp.dma_start(table[ds(c * CH, CH), :].rearrange("(b p) f -> p b f", p=P),
                                 T_[w][:, :, 0:width]).then_inc(s_stored[w], 16)
                    if p in DST_PASSES:
                        sp.dma_start(tab_dst[DST_PASSES.index(p)][ds(c * CH, CH), :].rearrange("(b p) f -> p b f", p=P),
                                     T_[w][:, :, width:width + F]).then_inc(s_stored2[w], 16)
                    yield
                chains(sp, body)
            for w in range(CHAINS):
                sp.wait_ge(s_stored[w], 16 * turns_of(w) * (END + 1))

        @block.gpsimd
        def _(pool):
            nc.gpsimd.memset(w2b[:, :], 0.0).then_inc(s_cst, 1)
            pool.wait_ge(s_cst, 1)
            nc.gpsimd.iota(iota_i[:, :], [[1, WIN]], base=0, channel_multiplier=0).then_inc(s_cst, 1)
            pool.wait_ge(s_cst, 2)
            nc.gpsimd.iota(eidx[:, :], [[P, TG]], base=(NG - SLOTS) * GE, channel_multiplier=1).then_inc(s_cst, 1)
            pool.wait_ge(s_cst, 3)
            nc.gpsimd.iota(two_i[:, :], [[0, 1]], base=-F, channel_multiplier=1).then_inc(s_cst, 1)
            pool.wait_ge(s_cst, 4)
            nc.gpsimd.memset(ident[:, :], 0.0).then_inc(s_cst, 1)
            pool.wait_ge(s_cst, 5)
            nc.gpsimd.memset(mean[:, :], 1.0 / F).then_inc(s_cst, 1)
            pool.wait_ge(s_cst, 6)
            nc.gpsimd.memset(rowsel[:, :, :], 0.0).then_inc(s_cst, 1)
            pool.wait_ge(s_cst, 7)
            nc.gpsimd.memset(rowsel_x[:, :], 0.0).then_inc(s_cst, 1)
            pool.wait_ge(s_cst, 8)
            nc.gpsimd.affine_select(out=ident[:, :], in_=ident[:, :], compare_op=ALU.not_equal, fill=1.0, base=0,
                                    pattern=[[-1, P]], channel_multiplier=1).then_inc(s_cst, 1)
            pool.wait_ge(s_cst, 9)
            nc.gpsimd.affine_select(out=rowsel[:, :, :], in_=rowsel[:, :, :],
                                    compare_op=ALU.not_equal, fill=1.0, base=-(ROWS - 2),
                                    pattern=[[-1, 2], [0, F]], channel_multiplier=1).then_inc(s_cst, 1)
            pool.wait_ge(s_cst, 10)
            nc.gpsimd.affine_select(out=rowsel_x[:, :], in_=rowsel_x[:, :],
                                    compare_op=ALU.not_equal, fill=1.0, base=-F,
                                    pattern=[[0, F]], channel_multiplier=1).then_inc(s_cst, 1)

            def gathers(p, R):
                table = tab_gate if p == GATE else tab[p]
                width = 2 * F if p == GATE else F
                with pool.Fori(0, R) as r:
                    q = pool.snap(r + R * p)
                    with pool.Fori(0, ITERS) as i:
                        for u in range(SLOTS):
                            wait_apart(pool, s_idx, q * (NG + SLOTS) + i * SLOTS + (u + 1))
                            for j in range(TG):
                                nc.gpsimd.indirect_dma_start(
                                    rows[:, u, j, 0:width], None, table,
                                    bass.IndirectOffsetOnAxis(idx[:, u, j:j + 1], 0)).then_inc(s_gather[u], 16)

            pool.wait_ge(s_rounds, 1)
            R = pool.value_load(rounds[0:1, 0:1], min_val=1, max_val=NP // WIN)
            for p in PASSES:
                for w in range(CHAINS):
                    pool.wait_ge(s_stored[w], 16 * turns_of(w) * (p + 1))
                gathers(p, R)

        @block.tensor
        def _(pe):
            mm = nc.tensor.matmul
            pe.wait_ge(s_w, 16 * (n_w - 1))
            pe.wait_ge(s_cst, 11)
            pe.wait_ge(s_x, 16)
            pe.wait_ge(s_prep, 2)

            def dst_rows(p, i, u, r, kq):
                s = u % SLOTS
                k = i * SLOTS + u
                pe.wait_ge(s_hot, kq * (NG + 1) + k + 1)
                for j in range(TG):
                    last = nc.tensor.transpose(ps_t[:, j * P:(j + 1) * P], hot[:, s, j, :], ident[:, :])
                last.then_inc(s_tp, 1)
                pe.wait_ge(s_tc, kq * (NG + 1) + k + 1)
                nth = i * (SLOTS // 2) + (u // 2 + 1)
                pe.wait_ge(s_win[u % 2], (kq * (NG // 2 + 1) + nth) * 16)
                if p == MLP:
                    pe.wait_ge(s_attr[u % 2], (r * (NG // 2 + 1) + nth) * 16)
                for j in range(TG):
                    last = mm(ps_e[:, u % 2, j * F:(j + 1) * F], hotT[:, j, :], win[:, u % 2, :],
                              start=True, stop=p == GATE)
                    if p == MLP:
                        last = mm(ps_e[:, u % 2, j * F:(j + 1) * F], attr[:, u % 2, j * P:(j + 1) * P], w1c[:, :],
                                  start=False, stop=True)
                last.then_inc(s_ex, 1)

            def sums(p, i, u, r, q):
                k = i * SLOTS + u
                if p == GATE:
                    pe.wait_ge(s_wh, q * NG + k + 1)
                elif p == MLP:
                    pe.wait_ge(s_relu, r * NG + k + 1)
                else:
                    pe.wait_ge(s_wh, (r + R * WEIGHTED.index(p)) * NG + k + 1)
                    pe.wait_ge(s_gather[u], (q * ITERS + i + 1) * (16 * TG))
                for j in range(TG):
                    lhs = (rows[:, u, j, F:2 * F] if p == GATE else act_out[:, u % 2, j, :] if p == MLP
                           else rows[:, u, j, 0:F])
                    rhs = hot[:, u, j, :] if p == MLP else whot[:, u % 2, j, :]
                    last = mm(ps_a[0:F, u % 2, 0:WIN], lhs, rhs, start=j == 0, stop=j == TG - 1)
                if p == GATE:
                    for j in range(TG):
                        last = mm(ps_a[F:F + 2, u % 2, 0:WIN], onesm[:, u % 2, j, :], hot[:, u, j, :],
                                  start=j == 0, stop=j == TG - 1)
                last.then_inc(s_agg, 1)
                if p == GCN1:
                    pe.wait_ge(s_lohi, r * NG + k + 1)
                    for j in range(TG):
                        last = mm(ps_h[:, 0:HI], lo_hot[:, j, :], hi_hot[:, j, :], start=j == 0, stop=j == TG - 1)
                    last.then_inc(s_hist, 1)

            def to_table(w, c, p, s_in, inb, weights, width):
                wait_apart(pe, s_in, made(s_in, p, c))
                for b in range(NB):
                    last = mm(blocks(B_[w], width)[:, b, :], inb[:, b * P:(b + 1) * P], weights, start=True, stop=True)
                return last

            def norm(w, c, p, cmat):
                wait_apart(pe, s_xin, made(s_xin, p, c))
                mm(A_[w][0:F, :], cmat, L_[w], start=True, stop=True).then_inc(s_xc, 1)
                yield
                wait_apart(pe, s_sq, made(s_sq, p, c))
                mm(B_[w][0:F, :], mean[:, :], S_[w], start=True, stop=True).then_inc(s_var, 1)
                yield

            def spread(w, c, which):
                mm(B_[w][0:F, :], rowsel[:, which, :], acc[0:ROWS, cols(c)], start=True, stop=True).then_inc(s_row, 1)

            def back(w, c, p):
                wait_apart(pe, s_tab, made(s_tab, p, c))
                for b in range(NB):
                    last = mm(A_[w][0:F, b * P:(b + 1) * P], T_[w][:, b, 0:F], ident[:, :], start=True, stop=True)
                last.then_inc(s_back, 1)

            def node(c, w, nth, p):
                eye = ident[0:F, 0:F]
                if p in (MLP, HOP1, HOP2, END):
                    wait_apart(pe, s_chunk, made(s_chunk, p, c))
                if p == GATE:
                    wait_apart(pe, s_xcopy, made(s_xcopy, p, c))
                    mm(A_[w][0:F, :], w_in[:, :], X_[w], start=True, stop=True).then_inc(s_mm, 1)
                    yield
                    to_table(w, c, p, s_emb, E_[w], wcat[:, 0:2 * F], 2 * F)
                    for b in range(NB):
                        last = mm(blocks(A_[w], F)[:, b, :], E_[w][:, b * P:(b + 1) * P], wcat[:, 2 * F:],
                                  start=True, stop=True)
                    last.then_inc(s_tabps, 1)
                elif p in (GCN1, GCN2):
                    to_table(w, c, p, s_emb, E_[w], gcn_w[:, p - 1, :], F).then_inc(s_tabps, 1)
                elif p == SUM:
                    yield from norm(w, c, p, center4[:, :])
                    wait_apart(pe, s_std, made(s_std, p, c))
                    spread(w, c, 0)
                    yield
                    to_table(w, c, p, s_y, E_[w], eye, F).then_inc(s_tabps, 1)
                elif p == MLP:
                    spread(w, c, 0)
                    yield
                    yield from norm(w, c, p, center[:, :])
                    to_table(w, c, p, s_y, E_[w], w1a[:, :], 2 * F).then_inc(s_tabps, 1)
                elif p == HOP1:
                    mm(A_[w][0:F, :], w2b[:, :], acc[0:F + 2, cols(c)], start=True, stop=True).then_inc(s_mm, 1)
                    mm(B_[w][0:F, :], rowsel_x[:, :], x[0:F + 1, cols(c)], start=True, stop=True).then_inc(s_row, 1)
                    yield
                    wait_apart(pe, s_xcopy, made(s_xcopy, p, c))
                    wait_apart(pe, s_agg0, made(s_agg0, p, c))
                    mm(A_[w][0:F, :], wu[:, 0, :], X_[w], start=True, stop=False)
                    mm(A_[w][0:F, :], wu[:, 1, :], E_[w], start=False, stop=True).then_inc(s_mm2, 1)
                    yield
                    yield from norm(w, c, p, center[:, :])
                    to_table(w, c, p, s_y, E_[w], eye, F).then_inc(s_tabps, 1)
                    yield
                    back(w, c, p)
                elif p == HOP2:
                    spread(w, c, 1)
                    yield
                    wait_apart(pe, s_y, made(s_y, p, c))
                    mm(A_[w][0:F, :], w3[:, 0, :], E_[w], start=True, stop=True).then_inc(s_mm, 1)
                    yield
                    to_table(w, c, p, s_leaky, L_[w], eye, F).then_inc(s_tabps, 1)
                    yield
                    back(w, c, p)
                else:
                    spread(w, c, 1)
                    yield
                    wait_apart(pe, s_agg0, made(s_agg0, p, c))
                    mm(A_[w][0:F, :], w3[:, 1, :], E_[w], start=True, stop=True).then_inc(s_mm, 1)
                    yield
                    yield from norm(w, c, p, center[:, :])
                    to_table(w, c, p, s_y, E_[w], eye, F).then_inc(s_tabps, 1)
                yield

            R = None
            for p in PASSES:
                if p > 0:
                    pe.wait_ge(s_accdone, p)
                chains(pe, lambda c, w, nth, p=p: node(c, w, nth, p))
                if R is None:
                    pe.wait_ge(s_rounds, 1)
                    R = pe.value_load(rounds[0:1, 0:1], min_val=1, max_val=NP // WIN)
                with pe.Fori(0, R) as r:
                    q = pe.snap(r + R * p)
                    kq = pe.snap(r + R * DST_PASSES.index(p)) if p in DST_PASSES else None
                    if p in DST_PASSES:
                        dst_rows(p, 0, 0, r, kq)
                    with pe.Fori(0, ITERS) as i:
                        for u in range(SLOTS):
                            if p in DST_PASSES:
                                dst_rows(p, i, u + 1, r, kq)
                            sums(p, i, u, r, q)
            pe.wait_ge(s_accdone, END)
            chains(pe, lambda c, w, nth: node(c, w, nth, END))

        @block.scalar
        def _(act):
            A = nc.scalar.activation
            act.wait_ge(s_w, 16 * (n_w - 1))
            R = None

            def load_dst(p, b_load, u, n_expr):
                act.dma_start(win[:, u % 2, :], tab_dst[DST_PASSES.index(p)][ds(b_load, P), :]).then_inc(s_win[u % 2], 16)
                if p == MLP:
                    act.dma_start(attr[:, u % 2, :], t["attrT"][:, ds(n_expr * GE, GE)]).then_inc(s_attr[u % 2], 16)

            def norm(w, c, p):
                act.wait_ge(s_xc, made(s_xc, p, c))
                A(S_[w], A_[w][0:F, :], ACT.Square).then_inc(s_sq, 1)
                yield
                act.wait_ge(s_var, made(s_var, p, c))
                A(V_[w], B_[w][0:F, :], ACT.Sqrt, bias=eps_col[:, :]).then_inc(s_std, 1)
                yield

            def node(c, w, nth, p):
                if p in (GATE, GCN1, GCN2, HOP1):
                    wait_apart(act, s_chunk, made(s_chunk, p, c))
                if p in (GATE, HOP1):
                    A(X_[w], x[0:F, cols(c)], ACT.Copy).then_inc(s_xcopy, 1)
                    yield
                if p == GATE:
                    act.wait_ge(s_mm, made(s_mm, p, c))
                    A(E_[w], A_[w][0:F, :], ACT.Identity, bias=bcol[:, 0:1]).then_inc(s_emb, 1)
                elif p in (GCN1, GCN2):
                    A(E_[w], acc[0:F, cols(c)], ACT.Relu, bias=bcol[:, p:p + 1]).then_inc(s_emb, 1)
                elif p == HOP1:
                    act.wait_ge(s_mm2, made(s_mm2, p, c))
                    A(S_[w], A_[w][0:F, :], ACT.Relu, bias=bcol[:, 4:5]).then_inc(s_h, 1)
                    yield
                    yield from norm(w, c, p)
                elif p in (SUM, MLP, END):
                    yield from norm(w, c, p)
                yield

            for p in PASSES + (END,):
                if p > 0:
                    act.wait_ge(s_accdone, p)
                if p == GCN2:
                    A(hist[:, :], hist[:, :], ACT.Sqrt).then_inc(s_outroot, 1)
                if p != HOP2:
                    chains(act, lambda c, w, nth, p=p: node(c, w, nth, p))
                if p == END:
                    break
                if R is None:
                    act.wait_ge(s_rounds, 1)
                    R = act.value_load(rounds[0:1, 0:1], min_val=1, max_val=NP // WIN)
                if p == GCN2:
                    with act.Fori(0, R) as r:
                        with act.Fori(0, SLICES) as i:
                            act.wait_ge(s_deg, r * SLICES + i + 1)
                            A(x[96:98, ds(i * SLICE, SLICE)], acc[96:98, ds(i * SLICE, SLICE)], ACT.Sqrt).then_inc(s_root, 1)
                if p not in DST_PASSES:
                    continue
                for w in range(CHAINS):
                    act.wait_ge(s_stored[w], 16 * turns_of(w) * (p + 1))
                    act.wait_ge(s_stored2[w], 16 * turns_of(w) * (DST_PASSES.index(p) + 1))
                with act.Fori(0, R) as r:
                    q = act.snap(r + R * p)
                    kq = act.snap(r + R * DST_PASSES.index(p))
                    wait_apart(act, s_base, q + 1)
                    for u in range(2):
                        b = act.value_load(base_i[0:1, 1 + u:2 + u], min_val=0, max_val=N)
                        load_dst(p, b, u, u)
                    act.wait_ge(s_tp, kq * (NG + 1) + 1)
                    A(hotT[:, :, :].rearrange("p a b -> p (a b)"), ps_t[:, :], ACT.Copy).then_inc(s_tc, 1)
                    with act.Fori(0, ITERS) as i:
                        for u in range(SLOTS):
                            k = i * SLOTS + u
                            b = act.value_load(base_i[0:1, ds(i * SLOTS + (u + 3), 1)], min_val=0, max_val=N)
                            act.wait_ge(s_ex, kq * (NG + 1) + k + 1)
                            load_dst(p, b, u, i * SLOTS + (u + 2))
                            act.wait_ge(s_tp, kq * (NG + 1) + k + 2)
                            A(hotT[:, :, :].rearrange("p a b -> p (a b)"), ps_t[:, :], ACT.Copy).then_inc(s_tc, 1)
                            if p == GATE:
                                act.wait_ge(s_logit, kq * NG + k + 1)
                                A(sig[:, u % 2, :], logit[:, u % 2, :], ACT.Sigmoid, bias=l2b[:, 0:1]).then_inc(s_sig, 1)
                            else:
                                act.wait_ge(s_pre, r * NG + k + 1)
                                A(act_out[:, u % 2, :, :], pre[:, :, :], ACT.Relu).then_inc(s_relu, 1)
                    for h in range(2):
                        act.wait_ge(s_win[h], (kq + 1) * (NG // 2 + 1) * 16)
                        if p == MLP:
                            act.wait_ge(s_attr[h], (r + 1) * ((NG // 2 + 1) * 16))

        @block.vector
        def _(dve):
            V = nc.vector
            dve.wait_ge(s_e, 48)
            g2 = rows[0:NG // 2, 0:2, :, :].rearrange("p a b c -> p a (b c)").bitcast(I32)
            V.tensor_reduce(low[:, :], g2, AX_X, ALU.min)
            V.tensor_reduce(high[:, :], g2, AX_X, ALU.max).then_inc(s_prep, 1)
            V.tensor_copy(dst[:, :], dloc[:, :].bitcast(I32))
            V.tensor_copy(gate[:, :], src[:, :])
            dve.drain()
            V.tensor_tensor(notself[:, :], gate[:, :], dst[:, :], ALU.not_equal)
            dve.drain()
            V.memset(gate[:, :], 0.0)
            dve.wait_ge(s_cst, 11)
            V.tensor_copy(iota[:, :], iota_i[:, :])
            V.tensor_copy(plus[:, :], two_i[:, :])
            V.memset(eps_col[:, :], EPS)
            for g in range(NG - SLOTS, NG):
                c0 = g * TG
                dve.drain()
                V.tensor_scalar(pad_ok[:, :], eidx[:, :], float(E - (g - (NG - SLOTS)) * GE), None, ALU.is_lt)
                dve.drain()
                V.tensor_scalar(pad_far[:, :], pad_ok[:, :], 1.0, FAR, ALU.subtract, ALU.mult)
                dve.drain()
                V.tensor_tensor(notself[:, c0:c0 + TG], notself[:, c0:c0 + TG], pad_ok[:, :], ALU.mult)
                V.tensor_tensor(dst[:, c0:c0 + TG], dst[:, c0:c0 + TG], pad_far[:, :], ALU.add)
            V.memset(dst[:, NG * TG:NGP * TG], -FAR)
            V.tensor_tensor(center[:, :], ident[0:F, 0:F], mean[:, :], ALU.subtract)
            dve.drain()
            V.tensor_scalar(center4[:, :], center[:, :], 0.25, None, ALU.mult)
            V.memset(onesm[:, :, :, :], 1.0)
            V.memset(base[:, :], 0.0)
            V.memset(zeros[:, :], 0.0)
            V.memset(acc[:, :], 0.0).then_inc(s_prep, 1)
            V.memset(x[F:P, :], 0.0)
            dve.drain()
            dve.wait_ge(s_span_in, 32)
            V.tensor_tensor(span[:, :], span[:, :], base0[:, :], ALU.subtract)
            dve.drain()
            V.tensor_reduce(spanm[:, :], span[:, :], AX_X, ALU.max)
            dve.drain()
            V.tensor_scalar(spanm[:, :], spanm[:, :], float(WIN), None, ALU.add)
            dve.drain()
            V.tensor_copy(rounds[:, :], spanm[:, :])
            dve.drain()
            V.tensor_scalar(rounds[:, :], rounds[:, :], WIN.bit_length() - 1, None, ALU.arith_shift_right)\
             .then_inc(s_rounds, 1)
            dve.wait_ge(s_w, 16 * (n_w - 1))
            dve.wait_ge(s_x, 16)
            dve.wait_ge(s_rounds, 1)
            R = dve.value_load(rounds[0:1, 0:1], min_val=1, max_val=NP // WIN)
            V.memset(token[:, :], 0.0).then_inc(s_chunk, CHAINS)

            def set_idx(k_expr, slot):
                V.tensor_copy(idx[:, slot, :], src[:, ds(k_expr, TG)]).then_inc(s_idx, 1)

            def norm_end(w, c, p, o):
                dve.wait_ge(s_std, made(s_std, p, c))
                V.reciprocal(L_[w], V_[w])
                yield
                dve.drain()
                return V.tensor_tensor(o, A_[w][0:F, :], L_[w], ALU.mult)

            def free_rows(w, c, p, nth):
                dve.wait_ge(s_tabps, made(s_tabps, p, c))
                if p > 0:
                    wait_apart(dve, s_stored[w], nth * 16 + 16 * turns_of(w) * p)
                    if p in DST_PASSES:
                        wait_apart(dve, s_stored2[w], nth * 16 + 16 * turns_of(w) * DST_PASSES.index(p))

            def each_node(v, width):
                return v.rearrange("p (a f) -> p a f", a=1).broadcast_to([P, NB, width])

            def clear(c):
                V.tensor_copy(acc[0:F, cols(c)], zeros[:, :])

            def node(c, w, nth, p):
                xc, ac = x[0:F, cols(c)], acc[0:F, cols(c)]
                A, B = A_[w][0:F, :], B_[w][0:F, :]
                if p == GATE:
                    free_rows(w, c, p, nth)
                    V.tensor_copy(T_[w][:, :, 0:2 * F], blocks(B_[w], 2 * F))
                    V.tensor_tensor(T_[w][:, :, 2 * F:], blocks(A_[w], F), each_node(l1b[:, :], F), ALU.add).then_inc(s_tab, 1)
                    V.scalar_tensor_tensor(xc, xc, 4.0, E_[w], ALU.mult, ALU.add)
                    yield
                elif p in (GCN1, GCN2):
                    free_rows(w, c, p, nth)
                    V.tensor_copy(T_[w][:, :, 0:F], blocks(B_[w], F)).then_inc(s_tab, 1)
                    V.tensor_tensor(xc, xc, E_[w], ALU.add)
                    clear(c)
                    yield
                elif p == SUM:
                    V.scalar_tensor_tensor(L_[w], ac, bcol[:, 3:4], xc, ALU.add, ALU.add).then_inc(s_xin, 1)
                    yield
                    yield from norm_end(w, c, p, xc)
                    yield
                    dve.drain()
                    dve.wait_ge(s_row, made(s_row, p, c))
                    V.tensor_tensor(E_[w], xc, B, ALU.mult).then_inc(s_y, 1)
                    clear(c)
                    yield
                    free_rows(w, c, p, nth)
                    V.tensor_copy(T_[w][:, :, 0:F], blocks(B_[w], F)).then_inc(s_tab, 1)
                    yield
                elif p == MLP:
                    dve.wait_ge(s_row, made(s_row, p, c))
                    V.tensor_tensor(S_[w], ac, B, ALU.mult)
                    yield
                    dve.drain()
                    V.tensor_tensor(L_[w], S_[w], xc, ALU.add).then_inc(s_xin, 1)
                    clear(c)
                    yield
                    (yield from norm_end(w, c, p, E_[w])).then_inc(s_y, 1)
                    yield
                    dve.drain()
                    V.tensor_copy(xc, E_[w])
                    free_rows(w, c, p, nth)
                    V.tensor_copy(T_[w][:, :, 0:F], blocks(B_[w], 2 * F)[:, :, 0:F])
                    V.tensor_tensor(T_[w][:, :, F:2 * F], blocks(B_[w], 2 * F)[:, :, F:], each_node(b1[:, :], F), ALU.add)\
                     .then_inc(s_tab, 1)
                    yield
                elif p == HOP1:
                    dve.wait_ge(s_row, made(s_row, p, c))
                    V.tensor_copy(V_[w], B)
                    yield
                    dve.drain()
                    V.tensor_tensor(E_[w], A, V_[w], ALU.mult).then_inc(s_agg0, 1)
                    yield
                    dve.wait_ge(s_h, made(s_h, p, c))
                    V.scalar_tensor_tensor(L_[w], xc, 2.0, S_[w], ALU.mult, ALU.add).then_inc(s_xin, 1)
                    yield
                    (yield from norm_end(w, c, p, E_[w])).then_inc(s_y, 1)
                    yield
                    dve.drain()
                    V.tensor_copy(xc, E_[w])
                    yield
                elif p == HOP2:
                    dve.wait_ge(s_row, made(s_row, p, c))
                    V.tensor_tensor(E_[w], ac, B, ALU.mult).then_inc(s_y, 1)
                    yield
                    dve.wait_ge(s_mm, made(s_mm, p, c))
                    V.tensor_scalar(S_[w], A, bcol[:, 5:6], None, ALU.add)
                    yield
                    dve.drain()
                    V.scalar_tensor_tensor(L_[w], S_[w], 0.01, S_[w], ALU.mult, ALU.max).then_inc(s_leaky, 1)
                    yield
                else:
                    dve.wait_ge(s_row, made(s_row, p, c))
                    V.tensor_tensor(E_[w], ac, B, ALU.mult).then_inc(s_agg0, 1)
                    yield
                    dve.wait_ge(s_mm, made(s_mm, p, c))
                    V.tensor_scalar(S_[w], A, bcol[:, 6:7], None, ALU.add)
                    yield
                    dve.drain()
                    V.scalar_tensor_tensor(V_[w], S_[w], 0.01, S_[w], ALU.mult, ALU.max)
                    yield
                    dve.drain()
                    V.tensor_tensor(L_[w], V_[w], xc, ALU.add).then_inc(s_xin, 1)
                    yield
                    (yield from norm_end(w, c, p, E_[w])).then_inc(s_y, 1)
                    yield
                    free_rows(w, c, p, nth)
                    V.tensor_copy(T_[w][:, :, 0:F], blocks(B_[w], F)).then_inc(s_tab, 1)
                    yield
                if p in (HOP1, HOP2):
                    free_rows(w, c, p, nth)
                    V.tensor_tensor(T_[w][:, :, 0:F], blocks(B_[w], F),
                                    inv_out[:, ds(c * NB, NB)].rearrange("p (b a) -> p b a", a=1).broadcast_to([P, NB, F]),
                                    ALU.mult).then_inc(s_tab, 1)
                    yield
                    wait_apart(dve, s_back, made(s_back, p, c))
                    V.tensor_copy(ac, A)
                    yield
                if w == 0:
                    dve.drain()
                if p == GATE:
                    dve.wait_ge(s_stored[w], nth * 16 + 16)
                    dve.wait_ge(s_stored2[w], nth * 16 + 16)
                V.memset(token[:, w:w + 1], 0.0).then_inc(s_chunk, 1)
                yield

            def onehot(o, k, weight=None):
                for j in range(TG):
                    if weight is None:
                        last = V.tensor_scalar(o[:, j, :], iota[:, :], dloc[:, ds(k * TG + j, 1)], None, ALU.is_equal)
                    else:
                        last = V.tensor_scalar(o[:, j, :], iota[:, :], dloc[:, ds(k * TG + j, 1)],
                                               weight[:, ds(k * TG + j, 1)], ALU.is_equal, ALU.mult)
                return last

            for p in PASSES + (END,):
                if p == HOP1:
                    dve.wait_ge(s_outroot, 1)
                    V.reciprocal(inv_out[:, :], hist[:, :])
                dve.drain()
                chains(dve, lambda c, w, nth, p=p: node(c, w, nth, p))
                if p == END:
                    break

                if p == GCN1:
                    for w in range(CHAINS):
                        dve.wait_ge(s_stored[w], 16 * turns_of(w) * (p + 1))
                g_rows = F + 2 if p == GATE else F
                dve.drain()
                V.tensor_copy(base[:, 1:1 + NG], base0[:, :])
                with dve.Fori(0, R) as r:
                    q = dve.snap(r + R * p)
                    kq = dve.snap(r + R * DST_PASSES.index(p)) if p in DST_PASSES else None
                    dve.drain()
                    V.tensor_tensor(dloc[:, :].rearrange("p (g t) -> p g t", t=TG),
                                    dst[:, :].rearrange("p (g t) -> p g t", t=TG),
                                    base[:, 1:1 + NGP].rearrange("p (g a) -> p g a", a=1).broadcast_to([P, NGP, TG]),
                                    ALU.subtract)
                    dve.drain()
                    V.tensor_copy(base_i[:, :], base[:, :]).then_inc(s_base, 1)
                    if p == GCN1:
                        V.memset(hist[:, :], 0.0)
                    V.memset(ps_a[:, 1, 0:WIN], 0.0).then_inc(s_agg, 1)
                    for u in range(SLOTS - 1):
                        set_idx(u * TG, u)
                    if p in DST_PASSES:
                        onehot(hot[:, 0, :, :], 0).then_inc(s_hot, 1)
                    wait_apart(dve, s_base, q + 1)
                    def group(i, u, q, r, kq):
                            k = i * SLOTS + u
                            b = dve.value_load(base_i[0:1, ds(k, 1)], min_val=0, max_val=N)
                            if p in DST_PASSES:
                                onehot(hot[:, (u + 1) % SLOTS, :, :], k + 1).then_inc(s_hot, 1)
                                dve.wait_ge(s_ex, kq * (NG + 1) + k + 1)
                                dve.wait_ge(s_gather[u], (q * ITERS + i + 1) * (16 * TG))
                                if p == MLP:
                                    dve.wait_ge(s_agg, q * (NG + 1) + k + 1)
                                last = V.tensor_tensor(pre[:, :, :], ps_e[:, u % 2, :].rearrange("p (t f) -> p t f", f=F),
                                                rows[:, u, :, 0:F], ALU.add)
                                if p == MLP:
                                    last.then_inc(s_pre, 1)
                                else:
                                    dve.drain()
                                    V.scalar_tensor_tensor(pre[:, :, :], pre[:, :, :], 0.0,
                                                           l2w[:, :].rearrange("p (a f) -> p a f", a=1).broadcast_to([P, TG, F]),
                                                           ALU.max, ALU.mult)
                                    dve.drain()
                                    V.tensor_reduce(logit[:, u % 2, :], pre[:, :, :], AX_X, ALU.add).then_inc(s_logit, 1)
                            dve.drain()
                            dve.wait_ge(s_agg, q * (NG + 1) + k + 1)
                            V.tensor_tensor(acc[0:g_rows, ds(b, WIN)], acc[0:g_rows, ds(b, WIN)],
                                            ps_a[0:g_rows, (u - 1) % 2, 0:WIN], ALU.add)
                            set_idx((k + SLOTS - 1) * TG, (u - 1) % SLOTS)
                            if p == GATE:
                                kk = k * TG
                                V.tensor_copy(onesm[:, u % 2, :, 1], notself[:, ds(kk, TG)])
                                V.tensor_scalar(inwin[:, :], dloc[:, ds(kk, TG)], 0.0, None, ALU.is_ge)
                                dve.drain()
                                V.scalar_tensor_tensor(inwin[:, :], dloc[:, ds(kk, TG)], float(WIN), inwin[:, :],
                                                       ALU.is_lt, ALU.mult)
                                dve.drain()
                                dve.wait_ge(s_sig, kq * NG + k + 1)
                                V.tensor_tensor(inwin[:, :], inwin[:, :], sig[:, u % 2, :], ALU.mult)
                                dve.drain()
                                V.tensor_tensor(gate[:, ds(kk, TG)], gate[:, ds(kk, TG)], inwin[:, :], ALU.add)
                                V.tensor_tensor(whot[:, u % 2, :, :], hot[:, u, :, :],
                                                sig[:, u % 2, :].rearrange("p (t a) -> p t a", a=1).broadcast_to([P, TG, WIN]),
                                                ALU.mult).then_inc(s_wh, 1)
                            elif p != MLP:
                                w = {GCN1: gate, GCN2: gate, SUM: None, HOP1: notself, HOP2: notself}[p]
                                onehot(whot[:, u % 2, :, :], k, w).then_inc(s_wh, 1)
                            if p == GCN1:
                                kk = k * TG
                                V.tensor_scalar(lo_i[:, :], src[:, ds(kk, TG)], P - 1, None, ALU.bitwise_and)
                                V.tensor_scalar(hi_i[:, :], src[:, ds(kk, TG)], P.bit_length() - 1, None, ALU.arith_shift_right)
                                dve.drain()
                                V.tensor_copy(lo[:, :], lo_i[:, :])
                                V.tensor_scalar(hi[:, :], notself[:, ds(kk, TG)], -1.0, -float(HI), ALU.add, ALU.mult)
                                dve.drain()
                                V.tensor_tensor(hi[:, :], hi[:, :], hi_i[:, :], ALU.add)
                                dve.drain()
                                V.tensor_tensor(lo_hot[:, :, :], iota[:, 0:P].rearrange("p (a n) -> p a n", a=1).broadcast_to([P, TG, P]),
                                                lo[:, :].rearrange("p (t a) -> p t a", a=1).broadcast_to([P, TG, P]), ALU.is_equal)
                                V.tensor_tensor(hi_hot[:, :, :], iota[:, 0:HI].rearrange("p (a n) -> p a n", a=1).broadcast_to([P, TG, HI]),
                                                hi[:, :].rearrange("p (t a) -> p t a", a=1).broadcast_to([P, TG, HI]), ALU.is_equal)\
                                 .then_inc(s_lohi, 1)
                                dve.wait_ge(s_hist, r * NG + k + 1)
                                V.tensor_tensor(hist[:, :], hist[:, :], ps_h[:, 0:HI], ALU.add)
                    with dve.Fori(0, SLICES) as i:
                        group(i, 0, q, r, kq)
                        if p == GCN2:
                            sl = ds(i * SLICE, SLICE)
                            V.tensor_scalar(acc[96:98, sl], acc[64:66, sl], plus[64:66, :], 1.0, ALU.add, ALU.max)\
                             .then_inc(s_deg, 1)
                            V.tensor_scalar(x[64:65, sl], acc[64:65, sl], 1e-6, None, ALU.add)
                        group(i, 1, q, r, kq)
                        if p == GCN2:
                            dve.drain()
                            V.reciprocal(x[64:65, sl], x[64:65, sl])
                        group(i, 2, q, r, kq)
                        if p == GCN2:
                            dve.wait_ge(s_root, r * SLICES + i + 1)
                            V.reciprocal(acc[96:98, sl], x[96:98, sl])
                            dve.drain()
                            V.tensor_scalar(x[96:98, sl], acc[64:66, sl], plus[64:66, :], 1.0, ALU.add, ALU.min)
                        group(i, 3, q, r, kq)
                        if p == GCN2:
                            dve.drain()
                            V.tensor_tensor(acc[96:98, sl], acc[96:98, sl], x[96:98, sl], ALU.mult)
                    if SLICES < ITERS:
                        with dve.Fori(SLICES, ITERS) as i:
                            for u in range(SLOTS):
                                group(i, u, q, r, kq)
                    b = dve.value_load(base_i[0:1, NG:NG + 1], min_val=0, max_val=N)
                    dve.drain()
                    dve.wait_ge(s_agg, (q + 1) * (NG + 1))
                    V.tensor_tensor(acc[0:g_rows, ds(b, WIN)], acc[0:g_rows, ds(b, WIN)],
                                    ps_a[0:g_rows, (SLOTS - 1) % 2, 0:WIN], ALU.add)
                    V.tensor_copy(idx[:, SLOTS - 1, :], src[:, 0:TG]).then_inc(s_idx, 1)
                    dve.drain()
                    V.tensor_scalar(base[:, 1:1 + NG], base[:, 1:1 + NG], float(WIN), float(N), ALU.add, ALU.min)
                if p == GCN1:
                    dve.drain()
                    V.tensor_scalar(hist[:, :], hist[:, :], 1.0, None, ALU.add)
                V.memset(inwin[:, 0:1], 0.0).then_inc(s_accdone, 1)


_W = ["L0_gnn_W_in", "L0_gnn_l1_W", "L0_gnn_l1_b", "L0_gnn_l2_W", "L0_gnn_l2_b", "L0_gnn_gcn_W",
      "L2_gnn_W1", "L2_gnn_b1", "L2_gnn_W2", "L2_gnn_b2", "L2_gnn_Wu", "L3_gnn_W1", "L3_gnn_W2"]


def kernel(**inputs):
    import numpy as np
    import concourse.bacc as bacc
    from concourse.bass_utils import run_bass_kernel_spmd

    a = {k: np.asarray(v) for k, v in inputs.items()}
    n, e = a["x"].shape[0], a["src"].shape[0]
    np_, ng, ngp = sizes(n, e)
    per = TG * P

    def cols(v, m, mode):
        return np.ascontiguousarray(np.pad(v, (0, m * per - e), mode=mode).reshape(-1, P).T)

    xT = np.zeros((F, np_), a["x"].dtype)
    xT[:, :n] = a["x"].T
    attrT = np.zeros((a["edge_attr_16"].shape[1], ngp * per), a["edge_attr_16"].dtype)
    attrT[:, :e] = a["edge_attr_16"].T
    arrays = {k: np.ascontiguousarray(a[k]) for k in _W}
    arrays["xT"] = xT
    arrays["attrT"] = attrT
    arrays["src_cols"] = cols(a["src"], ngp, "constant")
    arrays["dst_cols"] = cols(a["dst"], ngp, "edge")
    arrays["dst_groups"] = np.pad(a["dst"], (0, ng * per - e), mode="edge").reshape(ng // 2, 2 * per)
    arrays["bias_cols"] = np.ascontiguousarray(np.stack(
        [a["L0_gnn_b_in"], *a["L0_gnn_gcn_b"], a["L2_gnn_bu"], a["L3_gnn_b1"], a["L3_gnn_b2"]], axis=1))

    nc = bacc.Bacc("TRN2", target_bir_lowering=False, num_devices=1)
    t = {k: nc.dram_tensor(f"in_{k}", v.shape, mybir.dt.from_np(v.dtype), kind="ExternalInput").ap()
         for k, v in arrays.items()}
    t["n_nodes"], t["n_edges"] = n, e
    out = nc.dram_tensor("out_0", (np_, F), F32, kind="ExternalOutput").ap()
    gnn_kernel(nc, t, out)
    r = run_bass_kernel_spmd(nc, [{f"in_{k}": v for k, v in arrays.items()}], core_ids=[0])
    return r.results[0]["out_0"][:n]
```

```python
from contextlib import ExitStack, nullcontext

import concourse.bass as bass
from concourse import mybir

P = 128
F = 64
F32 = mybir.dt.float32
BF16 = mybir.dt.bfloat16
I32 = mybir.dt.int32
ALU = mybir.AluOpType
ACT = mybir.ActivationFunctionType
AX_X = mybir.AxisListType.X
ds = bass.ds

DA = 16
WIN = P - DA
TG = 8
SLOTS = 4
CH = 512
EPS = 1e-5
CHAINS = 4
ROWS = 98
PHASE = 8
LAG = 3
FAR = 1.0e6


def sizes(n_nodes, n_edges):
    np_ = -(-(n_nodes + WIN) // CH) * CH
    ng = -(-n_edges // (P * TG * SLOTS)) * SLOTS
    return np_, ng, ng + SLOTS


def gnn_kernel(nc, t, out):
    N, E = t["n_nodes"], t["n_edges"]
    NP, NG, NGP = sizes(N, E)
    NCH = NP // CH
    NB = CH // P
    HI = NP // P
    ITERS = NG // SLOTS
    GE = TG * P
    assert NCH <= ITERS and NG % PHASE == 0 and PHASE == 2 * SLOTS
    BODIES = NG // PHASE
    BESIDE = BODIES - LAG
    assert 0 < BESIDE <= NCH <= BESIDE + LAG

    ctx = ExitStack()
    with ctx:
        def sb(name, shape, dt=F32):
            return ctx.enter_context(nc.sbuf_tensor(name, shape, dt))

        def ps(name, shape, dt=F32):
            return ctx.enter_context(nc.psum_tensor(name, shape, dt))

        def sem(name):
            return ctx.enter_context(nc.semaphore(name))

        def dram(name, shape):
            return nc.dram_tensor(name, shape, F32, kind="Internal").ap()

        tab_gate = dram("tab_gate", [NP, 2 * F])
        tab_dst = [dram("tab_dst0", [NP, F]), dram("tab_dst2", [NP, F])]
        tab = [None] + [dram(f"tab{n}", [NP, F]) for n in range(1, 7)]
        span_dram = dram("span_dram", [2, NG])

        acc = sb("acc", [P, NP])
        x = sb("x", [P, NP])
        src = sb("src", [P, NGP * TG], I32)
        dst = sb("dst", [P, NGP * TG])
        dloc = sb("dloc", [P, NGP * TG])
        notself = sb("notself", [P, NGP * TG])
        gate = sb("gate", [P, NGP * TG])
        hist = sb("hist", [P, HI])
        inv_out = sb("inv_out", [P, HI])
        base = sb("base", [P, NGP + 1])
        base0 = sb("base0", [P, NG])
        base_i = sb("base_i", [P, NGP + 1], I32)
        spanm = sb("spanm", [P, 1])
        rounds = sb("rounds", [P, 2], I32)
        slack = sb("slack", [P, 1])
        low = sb("low", [NG // 2, 2])
        high = sb("high", [NG // 2, 2])
        pad_ok = sb("pad_ok", [P, TG])
        pad_far = sb("pad_far", [P, TG])
        zeros = sb("zeros", [F, CH])
        rank_i = sb("rank_i", [P, 1], I32)
        iota_i = sb("iota_i", [P, P], I32)
        iota = sb("iota", [P, P])
        eidx = sb("eidx", [P, TG], I32)
        ident = sb("ident", [P, P])
        center = sb("center", [F, F])
        center4 = sb("center4", [F, F])
        mean = sb("mean", [F, F])
        rowsel = sb("rowsel", [ROWS, 2, F])
        rowsel_x = sb("rowsel_x", [F + 1, F])
        plus = sb("plus", [P, 1])
        eps_col = sb("eps_col", [F, 1])

        token = sb("token", [1, CHAINS + 4])
        side_rows = sb("side_rows", [P, NB, 2 * F])
        idx = sb("idx", [P, SLOTS, TG], I32)
        rows = sb("rows", [P, SLOTS, TG, 2 * F])
        hot = sb("hot", [P, SLOTS, TG, P])
        whot = sb("whot", [P, 2, TG, P])
        hotT0 = sb("hotT0", [P, TG, P])
        pre = sb("pre", [P, TG, F])
        act_out = sb("act_out", [P, 2, TG, F])
        span = pre[:, :, :].rearrange("p a b -> p (a b)")[:, 0:NG]
        reach_i = act_out[:, 0, :, :].rearrange("p a b -> p (a b)")[:, 0:NG].bitcast(I32)
        logit = sb("logit", [P, 2, TG])
        sig = sb("sig", [P, 2, TG])
        inwin = sb("inwin", [P, TG])
        onesm = sb("onesm", [P, 2, TG, 2])
        win = sb("win", [P, 2, F])
        spare_t = sb("spare_t", [P, 2 * GE])
        hotT = [hotT0[:, :, :], spare_t[:, GE:2 * GE].rearrange("p (t e) -> p t e", t=TG)]
        lo_hot = spare_t[:, 0:GE // 2].bitcast(BF16).rearrange("p (t n) -> p t n", n=P)
        hi_hot = spare_t[:, GE:GE + TG * HI // 2].bitcast(BF16).rearrange("p (t n) -> p t n", n=HI)
        lo_i = sb("lo_i", [P, TG], I32)
        hi_i = sb("hi_i", [P, TG], I32)
        lo = sb("lo", [P, TG])
        hi = sb("hi", [P, TG])

        w_in = sb("w_in", [F + 1, F])
        wcat = sb("wcat", [F, 3 * F])
        gcn_w = sb("gcn_w", [F, 2, F])
        w1a = sb("w1a", [F, 2 * F])
        w2b = sb("w2b", [F + 2, F])
        wu = sb("wu", [F + 1, 2, F])
        w3 = sb("w3", [F, 2, F])
        bcol = sb("bcol", [F, 7])
        l2w = sb("l2w", [P, F])
        l2b = sb("l2b", [P, 1])
        l1b = sb("l1b", [P, 3 * F])
        b1 = sb("b1", [P, F])

        def halves(ring, slots):
            return [ring[:, n, h:h + TG // 2, :].rearrange("p a b -> p (a b)")
                    for n in range(slots) for h in (0, TG // 2)]
        spare = halves(hot, SLOTS) + halves(rows, SLOTS) + halves(whot, 2)
        assert len(spare) >= 4 * CHAINS and TG * P == 2 * CH
        T_ = [a[:, 0:NB * 3 * F].rearrange("p (b c) -> p b c", b=NB) for a in
              (hotT0[:, :, :].rearrange("p a b -> p (a b)"), spare_t[:, 0:GE], spare_t[:, GE:2 * GE],
               act_out[:, :, :, :].rearrange("p a b c -> p (a b c)"))]

        E_, S_, V_, L_ = ([spare[b * CHAINS + w][0:F, :] for w in range(CHAINS)] for b in range(4))
        ps_t = ps("ps_t", [P, 2 * 512])
        ps_e = ps("ps_e", [P, 2, 512])
        ps_a = ps("ps_a", [P, 2, 512])
        ps_hx = ps("ps_hx", [P, 2, 512])
        ps_h = ps_hx[:, 0, :]
        A_ = [ps_t[:, 0:512], ps_e[:, 0, :], ps_a[:, 0, :], ps_hx[:, 0, :]]
        B_ = [ps_t[:, 512:1024], ps_e[:, 1, :], ps_a[:, 1, :], ps_hx[:, 1, :]]

        BY_HOT, BY_ATTR, BY_WHOT = CHAINS, CHAINS + 1, CHAINS + 2
        hot_h, whot_h = halves(hot, 2), halves(whot, 2)
        for ring in (hot_h, [spare_t[:, 0:CH]] * 4, whot_h):
            for n, buf in enumerate((E_, S_, V_, L_)):
                buf.append(ring[n][0:F, :])
            T_.append(side_rows[:, :, :])
        A_ += [A_[0], ps_hx[:, 0, :], ps_hx[:, 0, :]]
        B_ += [B_[0], ps_hx[:, 1, :], ps_hx[:, 1, :]]

        def pair(w, h):
            return (B_, A_)[h][w][:, 0:6 * F].rearrange("p (b c) -> p b c", b=2)

        def blocks(bank, width):
            return bank[:, 0:NB * width].rearrange("p (b c) -> p b c", b=NB)

        s_w = sem("weights_loaded")
        s_x = sem("x_loaded")
        s_e = sem("edges_loaded")
        s_cst = sem("consts_made")
        s_clear = sem("acc_and_x_rows_zeroed")
        s_span_out = sem("span_stored")
        s_span_in = sem("span_loaded")
        s_prep = sem("prep_done")
        s_rounds = sem("rounds_known")
        s_base = sem("base_ready")
        s_idx = sem("idx_ready")
        s_gather = [sem(f"gathered{n}") for n in range(SLOTS)]
        s_hot = sem("hot_ready")
        s_wh = sem("lhs_or_onehot_ready")
        s_tp = sem("transposed")
        s_tc = sem("hotT_copied")
        s_ex = sem("expanded")
        s_win = [sem("win_loaded0"), sem("win_loaded1")]
        s_attr = [sem("attr_loaded0"), sem("attr_loaded1")]
        s_logit = sem("logit_ready")
        s_sig = sem("sig_ready")
        s_pre = sem("pre_ready")
        s_relu = sem("relu_ready")
        s_agg = sem("agg_done")
        s_lohi = sem("lohi_ready")
        s_hist = sem("hist_done")
        s_accdone = sem("pass_summed")
        s_emb = sem("node_emb")
        s_row = sem("node_row_spread")
        s_agg0 = sem("node_aggregate")
        s_mm = sem("node_product")
        s_mm2 = sem("node_update_product")
        s_h = sem("node_relu")
        s_leaky = sem("node_leaky")
        s_xin = sem("ln_in")
        s_xc = sem("ln_centered")
        s_sq = sem("ln_squared")
        s_var = sem("ln_var")
        s_std = sem("ln_std")
        s_y = sem("table_in")
        s_tabps = sem("node_tab_ps")
        s_tab = sem("node_tab_sb")
        s_back = sem("hs_transposed_back")
        s_chunk = sem("chunk_done")
        s_stored = [sem(f"tab_stored{w}") for w in range(CHAINS)]
        s_stored2 = [sem(f"dst_tab_stored{w}") for w in range(CHAINS)]
        s_final = sem("chunk_sums_final")
        s_side = sem("side_rows_stored")
        s_counted_back = sem("gather_counts_at_zero")
        s_deg = sem("deg_clamped")
        s_root = sem("deg_rooted")
        s_outroot = sem("out_degree_root")
        s_passed = {e.engine: sem(f"waits_passed_{n}") for n, e in
                    (("pe", nc.tensor), ("act", nc.scalar), ("dve", nc.vector), ("pool", nc.gpsimd))}

        block = ctx.enter_context(nc.Block())

        n_w = 22
        GATE, GCN1, GCN2, SUM, MLP, HOP1, HOP2 = range(7)
        PASSES = (GATE, GCN1, GCN2, SUM, MLP, HOP1, HOP2)
        END = len(PASSES)
        DST_PASSES = (GATE, MLP)
        ROOTS, COUNT = GCN1, GCN2
        WEIGHTED = (GATE, GCN1, GCN2, SUM, HOP1, HOP2)

        MADE = {
            s_emb: (GATE, GCN1, GCN2), s_row: (SUM, MLP, HOP1, HOP2, END), s_agg0: (HOP1, END),
            s_mm: (GATE, HOP1, HOP2, END), s_mm2: (HOP1,), s_h: (HOP1,), s_leaky: (HOP2,),
            s_xin: (SUM, MLP, HOP1, END), s_xc: (SUM, MLP, HOP1, END), s_sq: (SUM, MLP, HOP1, END),
            s_var: (SUM, MLP, HOP1, END), s_std: (SUM, MLP, HOP1, END),
            s_y: (SUM, MLP, HOP1, HOP2, END), s_tabps: (GATE,) + PASSES[1:] + (END,),
            s_tab: (GATE,) + PASSES[1:] + (END,), s_back: (HOP1, HOP2), s_chunk: (GATE,) + PASSES[1:] + (END,),
        }

        def made(name, p, c):
            return c + (sum(NCH for q in MADE[name] if q < p) + 1)

        def side_chain(p):
            return {GATE: BY_ATTR, MLP: BY_WHOT}.get(p, BY_HOT)

        def beside(eng, p, group, node):
            if group is not None:
                with eng.Fori(0, LAG) as i:
                    for u in range(PHASE):
                        group(i * 2 + u // SLOTS, u % SLOTS)
            with eng.Fori(0, BESIDE) as c:
                turn = node(c, side_chain(p), c, p + 1)
                for u in range(PHASE):
                    if group is not None:
                        group(c * 2 + (2 * LAG + u // SLOTS), u % SLOTS)
                    next(turn)

        def chains(eng, body, start=0, peel=False):
            def step(first, n, nth):
                turns = [body(first + w, w, nth) for w in range(n)]
                while turns:
                    turns = [g for g in turns if next(g, body) is not body]
            if start:
                assert NCH - start <= CHAINS
                return step(start, NCH - start, 0)
            if peel:
                step(0, CHAINS, 0)
            with eng.Fori(1 if peel else 0, NCH // CHAINS) as i:
                step(i * CHAINS, CHAINS, i)
            if NCH % CHAINS:
                step(NCH // CHAINS * CHAINS, NCH % CHAINS, NCH // CHAINS)

        def turns_of(w):
            return (NCH - w + CHAINS - 1) // CHAINS

        def stored_by(w, p, fast):
            if not fast:
                return 16 * turns_of(w) * (p + 1)
            return 16 * (turns_of(w) + p * (1 if w < NCH - BESIDE else 0))

        def stored_by2(w, p, fast):
            if p == GATE or not fast:
                return 16 * turns_of(w) * (DST_PASSES.index(p) + 1)
            return 16 * (turns_of(w) + (1 if w < NCH - BESIDE else 0))

        def side_by(p):
            return 16 * BESIDE * (p + (1 if p >= MLP else 0))

        def both(eng, regs, program):
            with eng.If(regs[1] == 1):
                program(True, 1)
            with eng.Else():
                program(False, regs[0])

        def each_round(eng, fast, R):
            return nullcontext(0) if fast else eng.Fori(0, R)

        def gathered(p, fast, i):
            return ((p * ITERS if fast else 0) + i + 1) * (16 * TG)

        def counts_at_zero(eng, fast, q):
            if not fast:
                wait_apart(eng, s_counted_back, q + 1)

        def counted(eng, fast, value):
            return value if fast else eng.snap(value)

        def wait_apart(eng, name, value):
            eng.wait_ge(name, value)
            eng.sem_inc(s_passed[eng.engine], 1)

        def cols(c):
            return ds(c * CH, CH)

        @block.sync
        def _(sp):
            def bc(ap, n):
                return ap.rearrange("(a n) -> a n", a=1).broadcast_to([P, n])
            l = [(w_in[0:F, :], t["L0_gnn_W_in"]), (wcat[:, 0:F], t["L0_gnn_l1_W"][0:F, :]),
                 (wcat[:, F:2 * F], t["L0_gnn_gcn_W"][0, :, :]), (wcat[:, 2 * F:], t["L0_gnn_l1_W"][F:2 * F, :]),
                 (gcn_w[:, 0, :], t["L0_gnn_gcn_W"][1, :, :]), (gcn_w[:, 1, :], t["L0_gnn_gcn_W"][2, :, :]),
                 (w1a[:, 0:F], t["L2_gnn_W1"][0:F, :]), (w1a[:, F:], t["L2_gnn_W1"][F:2 * F, :]),
                 (win[WIN:P, 0, :], t["L2_gnn_W1"][2 * F:2 * F + DA, :]),
                 (win[WIN:P, 1, :], t["L2_gnn_W1"][2 * F:2 * F + DA, :]), (w2b[0:F, :], t["L2_gnn_W2"]),
                 (w2b[F:F + 1, :], t["L2_gnn_b2"].rearrange("(a n) -> a n", a=1)),
                 (wu[0:F, 0, :], t["L2_gnn_Wu"][0:F, :]), (wu[0:F, 1, :], t["L2_gnn_Wu"][F:2 * F, :]),
                 (w3[:, 0, :], t["L3_gnn_W1"]), (w3[:, 1, :], t["L3_gnn_W2"]),
                 (bcol[:, :], t["bias_cols"]),
                 (l2w[:, :], bc(t["L0_gnn_l2_W"].rearrange("a b -> (a b)"), F)), (l2b[:, :], bc(t["L0_gnn_l2_b"], 1)),
                 (l1b[:, 2 * F:], bc(t["L0_gnn_l1_b"], F)), (b1[:, :], bc(t["L2_gnn_b1"], F))]
            sp.dma_start(x[0:F, :], t["xT"]).then_inc(s_x, 16)
            sp.wait_ge(s_cst, 3)
            for o, i in l:
                sp.dma_start(o, i).then_inc(s_w, 16)
            assert len(l) + 1 == n_w
            sp.wait_ge(s_prep, 1)
            sp.dma_start(span_dram[0, :].rearrange("(p k) -> p k", k=2), low[:, :]).then_inc(s_span_out, 16)
            sp.dma_start(span_dram[1, :].rearrange("(p k) -> p k", k=2), high[:, :]).then_inc(s_span_out, 16)
            sp.wait_ge(s_span_out, 32)
            sp.dma_start(base0[:, :], bc(span_dram[0, :], NG)).then_inc(s_span_in, 16)
            sp.dma_start(span[:, :], bc(span_dram[1, :], NG)).then_inc(s_span_in, 16)

            def body(c, w, nth, p):
                table = tab_gate if p == GATE else out if p == END else tab[p]
                width = 2 * F if p == GATE else F
                done, done2 = (s_stored[w], s_stored2[w]) if w < CHAINS else (s_side, s_side)
                sp.wait_ge(s_tab, made(s_tab, p, c))
                sp.dma_start(table[ds(c * CH, CH), :].rearrange("(b p) f -> p b f", p=P),
                             T_[w][:, :, 0:width]).then_inc(done, 16)
                if p in DST_PASSES:
                    sp.dma_start(tab_dst[DST_PASSES.index(p)][ds(c * CH, CH), :].rearrange("(b p) f -> p b f", p=P),
                                 T_[w][:, :, width:width + F]).then_inc(done2, 16)
                yield

            chains(sp, lambda c, w, nth: body(c, w, nth, GATE))
            sp.wait_ge(s_rounds, 1)
            regs = [sp.value_load(rounds[0:1, n:n + 1], min_val=1 - n, max_val=(N // WIN + 2, 1)[n]) for n in range(2)]

            def program(fast, R):
                for p in PASSES[1:] + (END,):
                    if fast:
                        with sp.Fori(0, BESIDE) as c:
                            next(body(c, side_chain(p - 1), c, p))
                    chains(sp, lambda c, w, nth, p=p: body(c, w, nth, p), start=BESIDE if fast else 0)
                for w in range(CHAINS):
                    sp.wait_ge(s_stored[w], stored_by(w, END, fast))
                if fast:
                    sp.wait_ge(s_side, side_by(END))
            both(sp, regs, program)

        @block.gpsimd
        def _(pool):
            nc.gpsimd.memset(w2b[:, :], 0.0).then_inc(s_cst, 1)
            pool.wait_ge(s_cst, 1)
            nc.gpsimd.memset(w_in[:, :], 0.0).then_inc(s_cst, 1)
            pool.wait_ge(s_cst, 2)
            nc.gpsimd.memset(wu[:, :, :], 0.0).then_inc(s_cst, 1)
            pool.wait_ge(s_cst, 3)
            nc.gpsimd.iota(iota_i[:, :], [[1, P]], base=0, channel_multiplier=0).then_inc(s_cst, 1)
            pool.wait_ge(s_cst, 4)
            nc.gpsimd.iota(eidx[:, :], [[P, TG]], base=(NG - SLOTS) * GE, channel_multiplier=1).then_inc(s_cst, 1)
            pool.wait_ge(s_cst, 5)
            nc.gpsimd.iota(rank_i[:, :], [[0, 1]], base=-F, channel_multiplier=1).then_inc(s_cst, 1)
            pool.wait_ge(s_cst, 6)
            nc.gpsimd.iota(reach_i.rearrange("p (a b) -> p a b", b=PHASE), [[CH, BODIES], [0, PHASE]],
                           base=-(LAG - 1) * CH, channel_multiplier=0).then_inc(s_cst, 1)
            pool.wait_ge(s_cst, 7)
            nc.gpsimd.memset(ident[:, :], 0.0).then_inc(s_cst, 1)
            pool.wait_ge(s_cst, 8)
            nc.gpsimd.memset(mean[:, :], 1.0 / F).then_inc(s_cst, 1)
            pool.wait_ge(s_cst, 9)
            nc.gpsimd.memset(rowsel[:, :, :], 0.0).then_inc(s_cst, 1)
            pool.wait_ge(s_cst, 10)
            nc.gpsimd.memset(rowsel_x[:, :], 0.0).then_inc(s_cst, 1)
            pool.wait_ge(s_cst, 11)
            nc.gpsimd.affine_select(out=ident[:, :], in_=ident[:, :], compare_op=ALU.not_equal, fill=1.0, base=0,
                                    pattern=[[-1, P]], channel_multiplier=1).then_inc(s_cst, 1)
            pool.wait_ge(s_cst, 12)
            nc.gpsimd.affine_select(out=rowsel[:, :, :], in_=rowsel[:, :, :],
                                    compare_op=ALU.not_equal, fill=1.0, base=-(ROWS - 2),
                                    pattern=[[-1, 2], [0, F]], channel_multiplier=1).then_inc(s_cst, 1)
            pool.wait_ge(s_cst, 13)
            nc.gpsimd.affine_select(out=rowsel_x[:, :], in_=rowsel_x[:, :],
                                    compare_op=ALU.not_equal, fill=1.0, base=-F,
                                    pattern=[[0, F]], channel_multiplier=1).then_inc(s_cst, 1)
            pool.wait_ge(s_cst, 14)
            nc.gpsimd.memset(x[F:P, :], 0.0).then_inc(s_clear, 1)
            pool.wait_ge(s_clear, 1)
            nc.gpsimd.memset(acc[:, :], 0.0).then_inc(s_clear, 1)
            pool.wait_ge(s_clear, 2)

            def gathers(p, fast, R):
                table = tab_gate if p == GATE else tab[p]
                width = 2 * F if p == GATE else F
                with each_round(pool, fast, R) as r:
                    q = counted(pool, fast, r + R * p)
                    with pool.Fori(0, ITERS) as i:
                        for u in range(SLOTS):
                            wait_apart(pool, s_idx, q * (NG + SLOTS) + i * SLOTS + (u + 1))
                            for j in range(TG):
                                nc.gpsimd.indirect_dma_start(
                                    rows[:, u, j, 0:width], None, table,
                                    bass.IndirectOffsetOnAxis(idx[:, u, j:j + 1], 0)).then_inc(s_gather[u], 16)
                    if not fast:
                        wait_apart(pool, s_agg, (q + 1) * (NG + 1))
                        for u in range(SLOTS):
                            pool.wait_ge(s_gather[u], ITERS * 16 * TG)
                        pool.inc_swdge_sem(s_gather, [ITERS * 16 * TG] * SLOTS, mode="sub")
                        pool.sem_inc(s_counted_back, 1)

            pool.wait_ge(s_rounds, 1)
            regs = [pool.value_load(rounds[0:1, n:n + 1], min_val=1 - n, max_val=(N // WIN + 2, 1)[n]) for n in range(2)]

            def program(fast, R):
                if not fast:
                    pool.sem_inc(s_counted_back, 1)
                for p in PASSES:
                    for w in range(CHAINS):
                        pool.wait_ge(s_stored[w], stored_by(w, p, fast))
                    if fast and p > 0:
                        pool.wait_ge(s_side, side_by(p))
                    gathers(p, fast, R)
            both(pool, regs, program)

        @block.tensor
        def _(pe):
            mm = nc.tensor.matmul
            pe.wait_ge(s_w, 16 * (n_w - 1))
            pe.wait_ge(s_cst, 14)
            pe.wait_ge(s_x, 16)
            pe.wait_ge(s_clear, 1)

            def transposes(i, u, kq):
                pe.wait_ge(s_hot, kq * (NG + 1) + (i * SLOTS + u + 1))
                for j in range(TG):
                    last = nc.tensor.transpose(ps_t[0:WIN, j * P:(j + 1) * P], hot[:, u % SLOTS, j, 0:WIN], ident[:, :])
                last.then_inc(s_tp, 1)

            def expand(p, i, u, r, kq):
                pe.wait_ge(s_tc, kq * (NG + 1) + (i * SLOTS + u + 1))
                nth = i * (SLOTS // 2) + (u // 2 + 1)
                pe.wait_ge(s_win[u % 2], (kq * (NG // 2 + 1) + nth) * 16)
                if p == MLP:
                    pe.wait_ge(s_attr[u % 2], (r * (NG // 2 + 1) + nth) * 16)
                depth = P if p == MLP else WIN
                for j in range(TG):
                    last = mm(ps_e[:, u % 2, j * F:(j + 1) * F], hotT[u % 2][0:depth, j, :], win[0:depth, u % 2, :],
                              start=True, stop=True)
                last.then_inc(s_ex, 1)

            def add_edges(u, lhs, rhs, m=0, rows=F):
                for j in range(TG):
                    last = mm(ps_a[m:m + rows, u % 2, 0:WIN], lhs(j), rhs(j), start=j == 0, stop=j == TG - 1)
                return last

            def message_sums(u, count):
                pe.wait_ge(s_relu, count)
                add_edges(u, lambda j: act_out[:, u % 2, j, :], lambda j: hot[:, u, j, 0:WIN]).then_inc(s_agg, 1)

            def sums(p, i, u, r, fast, nth_w):
                k = i * SLOTS + u
                pe.wait_ge(s_wh, nth_w * NG + k + 1)
                if p != GATE:
                    pe.wait_ge(s_gather[u], gathered(p, fast, i))
                first = F if p == GATE else 0
                last = add_edges(u, lambda j: rows[:, u, j, first:first + F], lambda j: whot[:, u % 2, j, 0:WIN])
                if p == GATE:
                    last = add_edges(u, lambda j: onesm[:, u % 2, j, :], lambda j: hot[:, u, j, 0:WIN], F, 2)
                last.then_inc(s_agg, 1)
                if p == COUNT:
                    pe.wait_ge(s_lohi, r * NG + k + 1)
                    for j in range(TG):
                        last = mm(ps_h[:, 0:HI], lo_hot[:, j, :], hi_hot[:, j, :], start=j == 0, stop=j == TG - 1)
                    last.then_inc(s_hist, 1)

            def to_table(w, c, p, s_in, inb, weights, width):
                wait_apart(pe, s_in, made(s_in, p, c))
                for b in range(NB):
                    last = mm(blocks(B_[w], width)[:, b, :], inb[:, b * P:(b + 1) * P], weights, start=True, stop=True)
                return last

            def norm(w, c, p, cmat):
                wait_apart(pe, s_xin, made(s_xin, p, c))
                mm(A_[w][0:F, :], cmat, L_[w], start=True, stop=True).then_inc(s_xc, 1)
                yield
                wait_apart(pe, s_sq, made(s_sq, p, c))
                mm(B_[w][0:F, :], mean[:, :], S_[w], start=True, stop=True).then_inc(s_var, 1)
                yield

            def spread(w, c, which):
                mm(B_[w][0:F, :], rowsel[:, which, :], acc[0:ROWS, cols(c)], start=True, stop=True).then_inc(s_row, 1)

            def back(w, c, p):
                wait_apart(pe, s_tab, made(s_tab, p, c))
                for b in range(NB):
                    last = mm(A_[w][0:F, b * P:(b + 1) * P], T_[w][:, b, 0:F], ident[:, :], start=True, stop=True)
                last.then_inc(s_back, 1)

            def node(c, w, nth, p):
                eye = ident[0:F, 0:F]
                if p in (MLP, HOP1, HOP2, END):
                    if w >= CHAINS:
                        wait_apart(pe, s_final, c + ((p - 1) * BESIDE + 1))
                    else:
                        wait_apart(pe, s_chunk, made(s_chunk, p, c))
                if p == GATE:
                    wait_apart(pe, s_chunk, made(s_chunk, p, c))
                    mm(A_[w][0:F, :], w_in[:, :], x[0:F + 1, cols(c)], start=True, stop=True).then_inc(s_mm, 1)
                    yield
                    wait_apart(pe, s_emb, made(s_emb, p, c))
                    for b in range(NB):
                        last = mm(pair(w, b // 2)[:, b % 2, :], E_[w][:, b * P:(b + 1) * P], wcat[:, :], start=True, stop=True)
                    last.then_inc(s_tabps, 1)
                    yield
                elif p in (GCN1, GCN2):
                    yield
                    to_table(w, c, p, s_emb, E_[w], gcn_w[:, p - 1, :], F).then_inc(s_tabps, 1)
                    for _ in range(7):
                        yield
                elif p == SUM:
                    yield
                    yield from norm(w, c, p, center4[:, :])
                    wait_apart(pe, s_std, made(s_std, p, c))
                    spread(w, c, 0)
                    yield
                    yield
                    to_table(w, c, p, s_y, E_[w], eye, F).then_inc(s_tabps, 1)
                    for _ in range(3):
                        yield
                elif p == MLP:
                    spread(w, c, 0)
                    yield
                    yield
                    yield from norm(w, c, p, center[:, :])
                    yield
                    to_table(w, c, p, s_y, E_[w], w1a[:, :], 2 * F).then_inc(s_tabps, 1)
                    for _ in range(3):
                        yield
                elif p == HOP1:
                    mm(A_[w][0:F, :], w2b[:, :], acc[0:F + 2, cols(c)], start=True, stop=True).then_inc(s_mm, 1)
                    mm(B_[w][0:F, :], rowsel_x[:, :], x[0:F + 1, cols(c)], start=True, stop=True).then_inc(s_row, 1)
                    yield
                    yield
                    wait_apart(pe, s_agg0, made(s_agg0, p, c))
                    mm(A_[w][0:F, :], wu[:, 0, :], x[0:F + 1, cols(c)], start=True, stop=False)
                    mm(A_[w][0:F, :], wu[0:F, 1, :], E_[w], start=False, stop=True).then_inc(s_mm2, 1)
                    yield
                    yield from norm(w, c, p, center[:, :])
                    to_table(w, c, p, s_y, E_[w], eye, F).then_inc(s_tabps, 1)
                    yield
                    back(w, c, p)
                    yield
                    yield
                elif p == HOP2:
                    spread(w, c, 1)
                    yield
                    yield
                    wait_apart(pe, s_y, made(s_y, p, c))
                    mm(A_[w][0:F, :], w3[:, 0, :], E_[w], start=True, stop=True).then_inc(s_mm, 1)
                    yield
                    yield
                    to_table(w, c, p, s_leaky, L_[w], eye, F).then_inc(s_tabps, 1)
                    yield
                    yield
                    back(w, c, p)
                    yield
                    yield
                else:
                    spread(w, c, 1)
                    yield
                    wait_apart(pe, s_agg0, made(s_agg0, p, c))
                    mm(A_[w][0:F, :], w3[:, 1, :], E_[w], start=True, stop=True).then_inc(s_mm, 1)
                    yield
                    yield
                    yield from norm(w, c, p, center[:, :])
                    yield
                    to_table(w, c, p, s_y, E_[w], eye, F).then_inc(s_tabps, 1)
                    yield
                    yield

            chains(pe, lambda c, w, nth: node(c, w, nth, GATE))
            pe.wait_ge(s_prep, 2)
            pe.wait_ge(s_rounds, 1)
            regs = [pe.value_load(rounds[0:1, n:n + 1], min_val=1 - n, max_val=(N // WIN + 2, 1)[n]) for n in range(2)]

            def program(fast, R):
                for p in PASSES:
                    with each_round(pe, fast, R) as r:
                        counts_at_zero(pe, fast, counted(pe, fast, r + R * p))
                        kq = counted(pe, fast, r + R * DST_PASSES.index(p) if p in DST_PASSES else 0)
                        nth_w = counted(pe, fast, r + R * WEIGHTED.index(p) if p in WEIGHTED else 0)
                        if p in DST_PASSES:
                            transposes(0, 0, kq)
                            expand(p, 0, 0, r, kq)

                        def group(i, u):
                            if p in DST_PASSES:
                                transposes(i, u + 1, kq)
                            if p == MLP:
                                message_sums((u - 1) % SLOTS, r * (NG + 1) + (i * SLOTS + u + 1))
                            if p in DST_PASSES:
                                expand(p, i, u + 1, r, kq)
                            if p != MLP:
                                sums(p, i, u, r, fast, nth_w)
                        if fast:
                            beside(pe, p, group, node)
                        else:
                            with pe.Fori(0, ITERS) as i:
                                for u in range(SLOTS):
                                    group(i, u)
                        if p == MLP:
                            message_sums(SLOTS - 1, (r + 1) * (NG + 1))
                    pe.wait_ge(s_accdone, p + 1)
                    chains(pe, lambda c, w, nth, p=p: node(c, w, nth, p + 1), start=BESIDE if fast else 0)
            both(pe, regs, program)

        @block.scalar
        def _(act):
            A = nc.scalar.activation
            act.dma_start(rows[0:NG // 2, 0:2, :, :].rearrange("p a b c -> p (a b c)").bitcast(I32),
                          t["dst_groups"]).then_inc(s_e, 16)
            act.dma_start(src[:, :], t["src_cols"]).then_inc(s_e, 16)
            act.dma_start(dloc[:, :].bitcast(I32), t["dst_cols"]).then_inc(s_e, 16)
            act.wait_ge(s_w, 16 * (n_w - 1))

            def load_dst(p, b_load, u, n_expr):
                act.dma_start(win[0:WIN, u % 2, :], tab_dst[DST_PASSES.index(p)][ds(b_load, WIN), :]).then_inc(s_win[u % 2], 16)
                if p == MLP:
                    act.dma_start(hotT[u % 2][WIN:P, :, :].rearrange("p a b -> p (a b)"),
                                  t["attrT"][:, ds(n_expr * GE, GE)]).then_inc(s_attr[u % 2], 16)

            def copy_transposed(u):
                A(hotT[u % 2][0:WIN, :, :].rearrange("p a b -> p (a b)"), ps_t[0:WIN, :], ACT.Copy).then_inc(s_tc, 1)

            def norm(w, c, p):
                act.wait_ge(s_xc, made(s_xc, p, c))
                A(S_[w], A_[w][0:F, :], ACT.Square).then_inc(s_sq, 1)
                yield
                act.wait_ge(s_var, made(s_var, p, c))
                A(V_[w], B_[w][0:F, :], ACT.Sqrt, bias=eps_col[:, :]).then_inc(s_std, 1)
                yield

            def node(c, w, nth, p):
                if p in (GCN1, GCN2):
                    if w >= CHAINS:
                        wait_apart(act, s_final, c + ((p - 1) * BESIDE + 1))
                    else:
                        wait_apart(act, s_chunk, made(s_chunk, p, c))
                if p in (GATE, HOP1):
                    yield
                if p == GATE:
                    act.wait_ge(s_mm, made(s_mm, p, c))
                    A(E_[w], A_[w][0:F, :], ACT.Identity, bias=bcol[:, 0:1]).then_inc(s_emb, 1)
                    yield
                elif p in (GCN1, GCN2):
                    A(E_[w], acc[0:F, cols(c)], ACT.Relu, bias=bcol[:, p:p + 1]).then_inc(s_emb, 1)
                    for _ in range(8):
                        yield
                elif p == HOP1:
                    yield
                    act.wait_ge(s_mm2, made(s_mm2, p, c))
                    A(S_[w], A_[w][0:F, :], ACT.Relu, bias=bcol[:, 4:5]).then_inc(s_h, 1)
                    yield
                    yield from norm(w, c, p)
                    for _ in range(3):
                        yield
                elif p == SUM:
                    yield
                    yield from norm(w, c, p)
                    for _ in range(5):
                        yield
                elif p == MLP:
                    yield
                    yield
                    yield from norm(w, c, p)
                    for _ in range(4):
                        yield
                elif p == END:
                    for _ in range(3):
                        yield
                    yield from norm(w, c, p)
                    for _ in range(3):
                        yield

            chains(act, lambda c, w, nth: node(c, w, nth, GATE))
            act.wait_ge(s_rounds, 1)
            regs = [act.value_load(rounds[0:1, n:n + 1], min_val=1 - n, max_val=(N // WIN + 2, 1)[n]) for n in range(2)]

            def root(nth, c):
                act.wait_ge(s_deg, nth + 1)
                A(x[96:98, cols(c)], acc[96:98, cols(c)], ACT.Sqrt).then_inc(s_root, 1)

            def program(fast, R):
                for p in PASSES:
                    if p in DST_PASSES:
                        for w in range(CHAINS):
                            act.wait_ge(s_stored[w], stored_by(w, p, fast))
                            act.wait_ge(s_stored2[w], stored_by2(w, p, fast))
                        if fast and p > 0:
                            act.wait_ge(s_side, side_by(p))
                        with each_round(act, fast, R) as r:
                            q = counted(act, fast, r + R * p)
                            kq = counted(act, fast, r + R * DST_PASSES.index(p))
                            wait_apart(act, s_base, q + 1)
                            for u in range(2):
                                b = act.value_load(base_i[0:1, 1 + u:2 + u], min_val=0, max_val=N)
                                load_dst(p, b, u, u)
                            act.wait_ge(s_tp, kq * (NG + 1) + 1)
                            copy_transposed(0)

                            def group(i, u):
                                k = i * SLOTS + u
                                b = act.value_load(base_i[0:1, ds(i * SLOTS + (u + 3), 1)], min_val=0, max_val=N)
                                act.wait_ge(s_ex, kq * (NG + 1) + k + 1)
                                load_dst(p, b, u, i * SLOTS + (u + 2))
                                act.wait_ge(s_tp, kq * (NG + 1) + k + 2)
                                copy_transposed(u + 1)
                                if p == GATE:
                                    act.wait_ge(s_logit, kq * NG + k + 1)
                                    A(sig[:, u % 2, :], logit[:, u % 2, :], ACT.Sigmoid, bias=l2b[:, 0:1]).then_inc(s_sig, 1)
                                else:
                                    act.wait_ge(s_pre, r * NG + k + 1)
                                    A(act_out[:, u % 2, :, :], pre[:, :, :], ACT.Relu).then_inc(s_relu, 1)
                            if fast:
                                beside(act, p, group, node)
                            else:
                                with act.Fori(0, ITERS) as i:
                                    for u in range(SLOTS):
                                        group(i, u)
                            for h in range(2):
                                act.wait_ge(s_win[h], (kq + 1) * (NG // 2 + 1) * 16)
                                if p == MLP:
                                    act.wait_ge(s_attr[h], (r + 1) * ((NG // 2 + 1) * 16))
                    elif fast and p == ROOTS:
                        with act.Fori(0, LAG) as i:
                            root(i, i)
                        with act.Fori(0, BESIDE) as c:
                            turn = node(c, side_chain(p), c, p + 1)
                            next(turn)
                            root(c + LAG, c + (NCH - BESIDE))
                            for _ in turn:
                                pass
                    elif fast:
                        if p + 1 != HOP2:
                            beside(act, p, None, node)
                    elif p == ROOTS:
                        with act.Fori(0, R) as r:
                            with act.Fori(0, NCH) as i:
                                root(r * NCH + i, i)
                    act.wait_ge(s_accdone, p + 1)
                    if p == COUNT:
                        A(hist[:, :], hist[:, :], ACT.Sqrt).then_inc(s_outroot, 1)
                    if p + 1 != HOP2:
                        chains(act, lambda c, w, nth, p=p: node(c, w, nth, p + 1), start=BESIDE if fast else 0)
            both(act, regs, program)

        @block.vector
        def _(dve):
            V = nc.vector
            V.memset(token[:, :], 0.0).then_inc(s_chunk, CHAINS)
            V.memset(l1b[:, 0:2 * F], 0.0)
            dve.wait_ge(s_e, 48)
            g2 = rows[0:NG // 2, 0:2, :, :].rearrange("p a b c -> p a (b c)").bitcast(I32)
            V.tensor_reduce(low[:, :], g2, AX_X, ALU.min)
            V.tensor_reduce(high[:, :], g2, AX_X, ALU.max).then_inc(s_prep, 1)
            V.tensor_copy(dst[:, :], dloc[:, :].bitcast(I32))
            V.tensor_copy(gate[:, :], src[:, :])
            dve.drain()
            V.tensor_tensor(notself[:, :], gate[:, :], dst[:, :], ALU.not_equal)
            dve.drain()
            V.memset(gate[:, :], 0.0)
            dve.wait_ge(s_cst, 14)
            V.tensor_copy(iota[:, :], iota_i[:, :])
            V.tensor_copy(plus[:, :], rank_i[:, :])
            V.memset(eps_col[:, :], EPS)
            for g in range(NG - SLOTS, NG):
                c0 = g * TG
                dve.drain()
                V.tensor_scalar(pad_ok[:, :], eidx[:, :], float(E - (g - (NG - SLOTS)) * GE), None, ALU.is_lt)
                dve.drain()
                V.tensor_scalar(pad_far[:, :], pad_ok[:, :], 1.0, FAR, ALU.subtract, ALU.mult)
                dve.drain()
                V.tensor_tensor(notself[:, c0:c0 + TG], notself[:, c0:c0 + TG], pad_ok[:, :], ALU.mult)
                V.tensor_tensor(dst[:, c0:c0 + TG], dst[:, c0:c0 + TG], pad_far[:, :], ALU.add)
            V.memset(dst[:, NG * TG:NGP * TG], -FAR)
            V.tensor_tensor(center[:, :], ident[0:F, 0:F], mean[:, :], ALU.subtract)
            dve.drain()
            V.tensor_scalar(center4[:, :], center[:, :], 0.25, None, ALU.mult).then_inc(s_prep, 1)
            V.memset(onesm[:, :, :, :], 1.0)
            V.memset(base[:, :], 0.0)
            V.memset(zeros[:, :], 0.0)
            dve.drain()
            dve.wait_ge(s_span_in, 32)
            V.tensor_tensor(span[:, :], span[:, :], base0[:, :], ALU.subtract)
            dve.drain()
            V.tensor_reduce(spanm[:, :], span[:, :], AX_X, ALU.max)
            dve.drain()
            V.tensor_copy(span[:, :], reach_i[:, :])
            dve.drain()
            V.tensor_tensor(span[:, :], base0[:, :], span[:, :], ALU.subtract)
            dve.drain()
            V.tensor_reduce(slack[:, :], span[:, :], AX_X, ALU.min)
            dve.drain()
            V.tensor_scalar(slack[:, :], slack[:, :], 0.0, None, ALU.is_ge)
            dve.drain()
            V.scalar_tensor_tensor(slack[:, :], spanm[:, :], float(WIN), slack[:, :], ALU.is_lt, ALU.mult)
            V.tensor_scalar(spanm[:, :], spanm[:, :], 1.0 / WIN, 1.0 + 0.5 / WIN, ALU.mult, ALU.add)
            dve.drain()
            V.tensor_copy(rounds[:, 1:2], slack[:, :])
            V.tensor_copy(rounds[:, 0:1], spanm[:, :]).then_inc(s_rounds, 1)
            dve.wait_ge(s_w, 16 * (n_w - 1))
            dve.wait_ge(s_x, 16)
            dve.wait_ge(s_rounds, 1)
            regs = [dve.value_load(rounds[0:1, n:n + 1], min_val=1 - n, max_val=(N // WIN + 2, 1)[n]) for n in range(2)]

            def set_idx(k_expr, slot):
                V.tensor_copy(idx[:, slot, :], src[:, ds(k_expr, TG)]).then_inc(s_idx, 1)

            def norm_end(w, c, p, o):
                dve.wait_ge(s_std, made(s_std, p, c))
                V.reciprocal(L_[w], V_[w])
                yield
                dve.drain()
                return V.tensor_tensor(o, A_[w][0:F, :], L_[w], ALU.mult)

            def free_rows(w, c, p, nth, fast):
                dve.wait_ge(s_tabps, made(s_tabps, p, c))
                if p == GATE:
                    if type(nth) is not int or nth > 0:
                        wait_apart(dve, s_stored[w], nth * 16)
                        wait_apart(dve, s_stored2[w], nth * 16)
                elif w < CHAINS:
                    wait_apart(dve, s_stored[w], nth * 16 + stored_by(w, p - 1, fast))
                    if p in DST_PASSES:
                        wait_apart(dve, s_stored2[w], nth * 16 + stored_by2(w, GATE, fast))

            def final(w, c, p):
                if w >= CHAINS:
                    dve.drain()
                    V.memset(token[:, CHAINS:CHAINS + 1], 0.0).then_inc(s_final, 1)

            def finish(w, c, p):
                dve.drain()
                if w >= CHAINS:
                    dve.wait_ge(s_side, side_by_chunk(p, c))
                V.memset(token[:, w:w + 1], 0.0).then_inc(s_chunk, 1)

            def side_by_chunk(p, c):
                per = 32 if p == MLP else 16
                return c * per + (side_by(p - 1) + per)

            def each_node(v, width):
                return v.rearrange("p (a f) -> p a f", a=1).broadcast_to([P, NB, width])

            def clear(c):
                V.tensor_copy(acc[0:F, cols(c)], zeros[:, :])

            def node(c, w, nth, p, fast=False):
                xc, ac = x[0:F, cols(c)], acc[0:F, cols(c)]
                A, B = A_[w][0:F, :], B_[w][0:F, :]
                final(w, c, p)
                if p == GATE:
                    free_rows(w, c, p, nth, fast)
                    for h in range(2):
                        last = V.tensor_tensor(T_[w][:, 2 * h:2 * h + 2, :], pair(w, h),
                                               l1b[:, :].rearrange("p (a f) -> p a f", a=1).broadcast_to([P, 2, 3 * F]), ALU.add)
                    last.then_inc(s_tab, 1)
                    V.scalar_tensor_tensor(xc, xc, 4.0, E_[w], ALU.mult, ALU.add)
                    finish(w, c, p)
                    yield
                elif p in (GCN1, GCN2):
                    yield
                    yield
                    free_rows(w, c, p, nth, fast)
                    V.tensor_copy(T_[w][:, :, 0:F], blocks(B_[w], F)).then_inc(s_tab, 1)
                    V.tensor_tensor(xc, xc, E_[w], ALU.add)
                    clear(c)
                    for _ in range(5):
                        yield
                    finish(w, c, p)
                    yield
                elif p == SUM:
                    V.scalar_tensor_tensor(L_[w], ac, bcol[:, 3:4], xc, ALU.add, ALU.add).then_inc(s_xin, 1)
                    yield
                    yield
                    yield
                    yield from norm_end(w, c, p, xc)
                    yield
                    dve.drain()
                    dve.wait_ge(s_row, made(s_row, p, c))
                    V.tensor_tensor(E_[w], xc, B, ALU.mult).then_inc(s_y, 1)
                    clear(c)
                    yield
                    free_rows(w, c, p, nth, fast)
                    V.tensor_copy(T_[w][:, :, 0:F], blocks(B_[w], F)).then_inc(s_tab, 1)
                    yield
                    finish(w, c, p)
                    yield
                elif p == MLP:
                    yield
                    dve.wait_ge(s_row, made(s_row, p, c))
                    V.tensor_tensor(S_[w], ac, B, ALU.mult)
                    dve.drain()
                    V.tensor_tensor(L_[w], S_[w], xc, ALU.add).then_inc(s_xin, 1)
                    clear(c)
                    yield
                    yield
                    yield
                    (yield from norm_end(w, c, p, E_[w])).then_inc(s_y, 1)
                    dve.drain()
                    V.tensor_copy(xc, E_[w])
                    yield
                    free_rows(w, c, p, nth, fast)
                    V.tensor_copy(T_[w][:, :, 0:F], blocks(B_[w], 2 * F)[:, :, 0:F])
                    V.tensor_tensor(T_[w][:, :, F:2 * F], blocks(B_[w], 2 * F)[:, :, F:], each_node(b1[:, :], F), ALU.add)\
                     .then_inc(s_tab, 1)
                    yield
                    finish(w, c, p)
                    yield
                elif p == HOP1:
                    yield
                    dve.wait_ge(s_row, made(s_row, p, c))
                    V.tensor_copy(V_[w], B)
                    dve.drain()
                    V.tensor_tensor(E_[w], A, V_[w], ALU.mult).then_inc(s_agg0, 1)
                    yield
                    yield
                    dve.wait_ge(s_h, made(s_h, p, c))
                    V.scalar_tensor_tensor(L_[w], xc, 2.0, S_[w], ALU.mult, ALU.add).then_inc(s_xin, 1)
                    yield
                    (yield from norm_end(w, c, p, E_[w])).then_inc(s_y, 1)
                    dve.drain()
                    V.tensor_copy(xc, E_[w])
                elif p == HOP2:
                    yield
                    dve.wait_ge(s_row, made(s_row, p, c))
                    V.tensor_tensor(E_[w], ac, B, ALU.mult).then_inc(s_y, 1)
                    yield
                    yield
                    dve.wait_ge(s_mm, made(s_mm, p, c))
                    V.tensor_scalar(S_[w], A, bcol[:, 5:6], None, ALU.add)
                    dve.drain()
                    V.scalar_tensor_tensor(L_[w], S_[w], 0.01, S_[w], ALU.mult, ALU.max).then_inc(s_leaky, 1)
                    yield
                    yield
                else:
                    yield
                    dve.wait_ge(s_row, made(s_row, p, c))
                    V.tensor_tensor(E_[w], ac, B, ALU.mult).then_inc(s_agg0, 1)
                    yield
                    dve.wait_ge(s_mm, made(s_mm, p, c))
                    V.tensor_scalar(S_[w], A, bcol[:, 6:7], None, ALU.add)
                    dve.drain()
                    V.scalar_tensor_tensor(V_[w], S_[w], 0.01, S_[w], ALU.mult, ALU.max)
                    dve.drain()
                    V.tensor_tensor(L_[w], V_[w], xc, ALU.add).then_inc(s_xin, 1)
                    yield
                    yield
                    yield
                    (yield from norm_end(w, c, p, E_[w])).then_inc(s_y, 1)
                    yield
                    free_rows(w, c, p, nth, fast)
                    V.tensor_copy(T_[w][:, :, 0:F], blocks(B_[w], F)).then_inc(s_tab, 1)
                    finish(w, c, p)
                    yield
                if p in (HOP1, HOP2):
                    if p == HOP1:
                        yield
                    free_rows(w, c, p, nth, fast)
                    V.tensor_tensor(T_[w][:, :, 0:F], blocks(B_[w], F),
                                    inv_out[:, ds(c * NB, NB)].rearrange("p (b a) -> p b a", a=1).broadcast_to([P, NB, F]),
                                    ALU.mult).then_inc(s_tab, 1)
                    if p == HOP2:
                        yield
                    yield
                    wait_apart(dve, s_back, made(s_back, p, c))
                    V.tensor_copy(ac, A)
                    finish(w, c, p)
                    yield

            def onehot(o, k, weight=None):
                for j in range(TG):
                    if weight is None:
                        last = V.tensor_scalar(o[:, j, 0:WIN], iota[:, 0:WIN], dloc[:, ds(k * TG + j, 1)], None, ALU.is_equal)
                    else:
                        last = V.tensor_scalar(o[:, j, 0:WIN], iota[:, 0:WIN], dloc[:, ds(k * TG + j, 1)],
                                               weight[:, ds(k * TG + j, 1)], ALU.is_equal, ALU.mult)
                return last

            def start_round(p, fast, r, q):
                for u in range(SLOTS - 1):
                    set_idx(u * TG, u)
                dve.drain()
                V.tensor_tensor(dloc[:, :].rearrange("p (g t) -> p g t", t=TG),
                                dst[:, :].rearrange("p (g t) -> p g t", t=TG),
                                base[:, 1:1 + NGP].rearrange("p (g a) -> p g a", a=1).broadcast_to([P, NGP, TG]),
                                ALU.subtract)
                dve.drain()
                V.tensor_copy(base_i[:, :], base[:, :]).then_inc(s_base, 1)
                if p == COUNT:
                    V.memset(hist[:, :], 0.0)
                if p == MLP:
                    wait_apart(dve, s_stored[CHAINS - 1], stored_by(CHAINS - 1, p, fast))
                    wait_apart(dve, s_stored2[CHAINS - 1], stored_by2(CHAINS - 1, p, fast))
                    V.memset(hot[:, SLOTS - 1, :, :], 0.0)
                    V.memset(act_out[:, 1, :, :], 0.0).then_inc(s_relu, 1)
                else:
                    V.memset(ps_a[:, 1, 0:WIN], 0.0).then_inc(s_agg, 1)
                if p in DST_PASSES:
                    onehot(hot[:, 0, :, :], 0).then_inc(s_hot, 1)
                wait_apart(dve, s_base, q + 1)

            def end_round(p, fast, q, g_rows):
                b = dve.value_load(base_i[0:1, NG:NG + 1], min_val=0, max_val=N)
                dve.drain()
                dve.wait_ge(s_agg, (q + 1) * (NG + 1))
                V.tensor_tensor(acc[0:g_rows, ds(b, WIN)], acc[0:g_rows, ds(b, WIN)],
                                ps_a[0:g_rows, (SLOTS - 1) % 2, 0:WIN], ALU.add)
                V.tensor_copy(idx[:, SLOTS - 1, :], src[:, 0:TG]).then_inc(s_idx, 1)
                if not fast:
                    dve.drain()
                    V.tensor_scalar(base[:, 1:1 + NG], base[:, 1:1 + NG], float(WIN), float(N), ALU.add, ALU.min)

            def roots(c, nth):
                sl = cols(c)
                V.tensor_scalar(acc[96:98, sl], acc[64:66, sl], plus[64:66, :], 1.0, ALU.add, ALU.max).then_inc(s_deg, 1)
                V.tensor_scalar(x[64:65, sl], acc[64:65, sl], 1e-6, None, ALU.add)
                yield
                dve.drain()
                V.reciprocal(x[64:65, sl], x[64:65, sl])
                yield
                dve.wait_ge(s_root, nth + 1)
                V.reciprocal(acc[96:98, sl], x[96:98, sl])
                dve.drain()
                V.tensor_scalar(x[96:98, sl], acc[64:66, sl], plus[64:66, :], 1.0, ALU.add, ALU.min)
                yield
                dve.drain()
                V.tensor_tensor(acc[96:98, sl], acc[96:98, sl], x[96:98, sl], ALU.mult)
                yield

            def edge_pass(p, fast, R):
                if p == COUNT:
                    for w in range(CHAINS):
                        dve.wait_ge(s_stored[w], stored_by(w, p, fast))
                g_rows = F + 2 if p == GATE else F
                with each_round(dve, fast, R) as r:
                    q = counted(dve, fast, r + R * p)
                    kq = counted(dve, fast, r + R * DST_PASSES.index(p)) if p in DST_PASSES else 0
                    start_round(p, fast, r, q)
                    counts_at_zero(dve, fast, q)

                    def group(i, u):
                        k = i * SLOTS + u
                        b = dve.value_load(base_i[0:1, ds(k, 1)], min_val=0, max_val=N)
                        if p in DST_PASSES:
                            onehot(hot[:, (u + 1) % SLOTS, :, :], k + 1).then_inc(s_hot, 1)
                            dve.wait_ge(s_ex, kq * (NG + 1) + k + 1)
                            dve.wait_ge(s_gather[u], gathered(p, fast, i))
                            if p == MLP:
                                dve.wait_ge(s_relu, r * (NG + 1) + k + 1)
                            last = V.tensor_tensor(pre[:, :, :], ps_e[:, u % 2, :].rearrange("p (t f) -> p t f", f=F),
                                            rows[:, u, :, 0:F], ALU.add)
                            if p == MLP:
                                last.then_inc(s_pre, 1)
                            else:
                                dve.drain()
                                V.scalar_tensor_tensor(pre[:, :, :], pre[:, :, :], 0.0,
                                                       l2w[:, :].rearrange("p (a f) -> p a f", a=1).broadcast_to([P, TG, F]),
                                                       ALU.max, ALU.mult)
                                dve.drain()
                                V.tensor_reduce(logit[:, u % 2, :], pre[:, :, :], AX_X, ALU.add).then_inc(s_logit, 1)
                        dve.drain()
                        dve.wait_ge(s_agg, q * (NG + 1) + k + 1)
                        V.tensor_tensor(acc[0:g_rows, ds(b, WIN)], acc[0:g_rows, ds(b, WIN)],
                                        ps_a[0:g_rows, (u - 1) % 2, 0:WIN], ALU.add)
                        set_idx((k + SLOTS - 1) * TG, (u - 1) % SLOTS)
                        if p == GATE:
                            kk = k * TG
                            V.tensor_copy(onesm[:, u % 2, :, 1], notself[:, ds(kk, TG)])
                            V.tensor_scalar(inwin[:, :], dloc[:, ds(kk, TG)], 0.0, None, ALU.is_ge)
                            dve.drain()
                            V.scalar_tensor_tensor(inwin[:, :], dloc[:, ds(kk, TG)], float(WIN), inwin[:, :],
                                                   ALU.is_lt, ALU.mult)
                            dve.drain()
                            dve.wait_ge(s_sig, kq * NG + k + 1)
                            V.tensor_tensor(inwin[:, :], inwin[:, :], sig[:, u % 2, :], ALU.mult)
                            dve.drain()
                            V.tensor_tensor(gate[:, ds(kk, TG)], gate[:, ds(kk, TG)], inwin[:, :], ALU.add)
                            V.tensor_tensor(whot[:, u % 2, :, 0:WIN], hot[:, u, :, 0:WIN],
                                            sig[:, u % 2, :].rearrange("p (t a) -> p t a", a=1).broadcast_to([P, TG, WIN]),
                                            ALU.mult).then_inc(s_wh, 1)
                        elif p != MLP:
                            w = {GCN1: gate, GCN2: gate, SUM: None, HOP1: notself, HOP2: notself}[p]
                            onehot(whot[:, u % 2, :, :], k, w).then_inc(s_wh, 1)
                        if p == COUNT:
                            kk = k * TG
                            V.tensor_scalar(lo_i[:, :], src[:, ds(kk, TG)], P - 1, None, ALU.bitwise_and)
                            V.tensor_scalar(hi_i[:, :], src[:, ds(kk, TG)], P.bit_length() - 1, None, ALU.arith_shift_right)
                            dve.drain()
                            V.tensor_copy(lo[:, :], lo_i[:, :])
                            V.tensor_scalar(hi[:, :], notself[:, ds(kk, TG)], -1.0, -float(HI), ALU.add, ALU.mult)
                            dve.drain()
                            V.tensor_tensor(hi[:, :], hi[:, :], hi_i[:, :], ALU.add)
                            dve.drain()
                            for o, v, n in ((lo_hot, lo, P), (hi_hot, hi, HI)):
                                last = V.tensor_tensor(
                                    o[:, :, :], iota[:, 0:n].rearrange("p (a n) -> p a n", a=1).broadcast_to([P, TG, n]),
                                    v[:, :].rearrange("p (t a) -> p t a", a=1).broadcast_to([P, TG, n]), ALU.is_equal)
                            last.then_inc(s_lohi, 1)
                            dve.wait_ge(s_hist, r * NG + k + 1)
                            V.tensor_tensor(hist[:, :], hist[:, :], ps_h[:, 0:HI], ALU.add)

                    if fast and p != ROOTS:
                        beside(dve, p, group, lambda c, w, nth, p: node(c, w, nth, p, True))
                    elif fast:
                        with dve.Fori(0, LAG) as i:
                            part = roots(i, i)
                            for u in range(PHASE):
                                group(i * 2 + u // SLOTS, u % SLOTS)
                                if u % 2:
                                    next(part)
                        with dve.Fori(0, BESIDE) as c:
                            part = roots(c + (NCH - BESIDE), c + LAG)
                            turn = node(c, side_chain(p), c, p + 1, True)
                            for u in range(PHASE):
                                group(c * 2 + (2 * LAG + u // SLOTS), u % SLOTS)
                                next(turn)
                                if u % 2:
                                    next(part)
                    elif p == ROOTS:
                        with dve.Fori(0, NCH) as i:
                            part = roots(i, r * NCH + i)
                            for u in range(SLOTS):
                                group(i, u)
                                next(part)
                        if NCH < ITERS:
                            with dve.Fori(NCH, ITERS) as i:
                                for u in range(SLOTS):
                                    group(i, u)
                    else:
                        with dve.Fori(0, ITERS) as i:
                            for u in range(SLOTS):
                                group(i, u)
                    end_round(p, fast, q, g_rows)
                if not fast:
                    dve.drain()
                    V.tensor_copy(base[:, 1:1 + NG], base0[:, :])
                if p == COUNT:
                    dve.drain()
                    V.tensor_scalar(hist[:, :], hist[:, :], 1.0, None, ALU.add)
                V.memset(inwin[:, 0:1], 0.0).then_inc(s_accdone, 1)

            chains(dve, lambda c, w, nth: node(c, w, nth, GATE), peel=True)
            V.tensor_copy(base[:, 1:1 + NG], base0[:, :])
            dve.wait_ge(s_clear, 2)

            def program(fast, R):
                for p in PASSES:
                    edge_pass(p, fast, R)
                    if p == SUM:
                        dve.wait_ge(s_outroot, 1)
                        V.reciprocal(inv_out[:, :], hist[:, :])
                    dve.drain()
                    chains(dve, lambda c, w, nth, p=p: node(c, w, nth, p + 1, fast), start=BESIDE if fast else 0)
            both(dve, regs, program)


_W = ["L0_gnn_W_in", "L0_gnn_l1_W", "L0_gnn_l1_b", "L0_gnn_l2_W", "L0_gnn_l2_b", "L0_gnn_gcn_W",
      "L2_gnn_W1", "L2_gnn_b1", "L2_gnn_W2", "L2_gnn_b2", "L2_gnn_Wu", "L3_gnn_W1", "L3_gnn_W2"]


def kernel(**inputs):
    import numpy as np
    import concourse.bacc as bacc
    from concourse.bass_utils import run_bass_kernel_spmd

    a = {k: np.asarray(v) for k, v in inputs.items()}
    n, e = a["x"].shape[0], a["src"].shape[0]
    np_, ng, ngp = sizes(n, e)
    per = TG * P

    def cols(v, m, mode):
        return np.ascontiguousarray(np.pad(v, (0, m * per - e), mode=mode).reshape(-1, P).T)

    xT = np.zeros((F, np_), a["x"].dtype)
    xT[:, :n] = a["x"].T
    attrT = np.zeros((a["edge_attr_16"].shape[1], ngp * per), a["edge_attr_16"].dtype)
    attrT[:, :e] = a["edge_attr_16"].T
    arrays = {k: np.ascontiguousarray(a[k]) for k in _W}
    arrays["xT"] = xT
    arrays["attrT"] = attrT
    arrays["src_cols"] = cols(a["src"], ngp, "constant")
    arrays["dst_cols"] = cols(a["dst"], ngp, "edge")
    arrays["dst_groups"] = np.pad(a["dst"], (0, ng * per - e), mode="edge").reshape(ng // 2, 2 * per)
    arrays["bias_cols"] = np.ascontiguousarray(np.stack(
        [a["L0_gnn_b_in"], *a["L0_gnn_gcn_b"], a["L2_gnn_bu"], a["L3_gnn_b1"], a["L3_gnn_b2"]], axis=1))

    nc = bacc.Bacc("TRN2", target_bir_lowering=False, num_devices=1)
    t = {k: nc.dram_tensor(f"in_{k}", v.shape, mybir.dt.from_np(v.dtype), kind="ExternalInput").ap()
         for k, v in arrays.items()}
    t["n_nodes"], t["n_edges"] = n, e
    out = nc.dram_tensor("out_0", (np_, F), F32, kind="ExternalOutput").ap()
    gnn_kernel(nc, t, out)
    r = run_bass_kernel_spmd(nc, [{f"in_{k}": v for k, v in arrays.items()}], core_ids=[0])
    return r.results[0]["out_0"][:n]
```
